# Optimizing a Trainium2 kernel written in Bass

```python
import numpy as np
import jax
import jax.numpy as jnp

def _softmax(x, axis=-1):
    return jax.nn.softmax(x, axis=axis)

def _gelu(x):
    return jax.nn.gelu(x, approximate=True)

def _silu(x):
    return jax.nn.silu(x)

def _sigmoid(x):
    return jax.nn.sigmoid(x)

def _layernorm(x, axis=-1, eps=1e-05):
    m = jnp.mean(x, axis=axis, keepdims=True)
    v = jnp.var(x, axis=axis, keepdims=True)
    return (x - m) / jnp.sqrt(v + eps)

def _scatter_add(tgt, idx, src, axis=0):
    return tgt.at[idx].add(src)

def _segment_sum(src, seg, n):
    return jax.ops.segment_sum(src, seg, n)
kernel_name = 'mk_flamingo_gated_d1_seqx_r8_f49a71'

def setup_inputs(seed: int=0):
    np.random.seed(seed)
    _w = jnp.asarray

    def _rec_inputs():
        import jax
        import jax.numpy as jnp
        _rk = jax.random.key(seed)
        x = 7.22e-05 + 1 * jax.random.normal(jax.random.fold_in(_rk, 1), (32, 64, 128), jnp.float32)
        _lenS = 64 - jax.random.randint(jax.random.fold_in(_rk, 7), (32,), 0, max(1, 64 // 4) + 1, jnp.int32)
        _lenS2 = 64 - jax.random.randint(jax.random.fold_in(_rk, 8), (32,), 0, max(1, 64 // 4) + 1, jnp.int32)
        _ctx_1024P = jax.random.normal(jax.random.fold_in(_rk, 11), (32, 16, 128), jnp.float32)
        _ctx_1024c = jax.random.dirichlet(jax.random.fold_in(_rk, 511), 0.3 * jnp.ones((16,), jnp.float32), (32, 64))
        _ctx_1024t = jnp.einsum('bsk,bkd->bsd', _ctx_1024c, _ctx_1024P)
        _ctx_1024t = _ctx_1024t * jax.lax.rsqrt(jnp.mean(jnp.square(_ctx_1024t)) + 1e-12) * 0.953939
        ctx_1024 = 4.13588e-05 + 0.999923 * (_ctx_1024t + 0.3 * jax.random.normal(jax.random.fold_in(_rk, 611), (32, 64, 128), jnp.float32))
        _g = jax.random.normal(jax.random.fold_in(_rk, 9001), (2, 1), jnp.float32)
        _g = jnp.sign(_g) * jnp.maximum(jnp.abs(_g), 1.0) + (_g == 0) * 1.0
        g_xattn = _g[0]
        g_ffn = _g[1]
        return (x, ctx_1024, g_xattn, g_ffn)
    x, ctx_1024, g_xattn, g_ffn = _rec_inputs()

    def _L0_xattn_setup():
        import jax, jax.numpy as jnp
        import numpy as np
        EMBED = 128
        HEADS = 16
        HEAD_DIM = EMBED // HEADS
        WINDOW = 128
        HALF = WINDOW // 2
        SCALE = HEAD_DIM ** (-0.5)
        B, T = (2, 512)

        def _sliding_window_attn(q, k, v):
            Bq, H, Tq, D = q.shape
            Bk = HALF
            nb = Tq // Bk
            qb = q.reshape(Bq, H, nb, Bk, D)

            def ctx(x):
                xb = x.reshape(Bq, H, nb, Bk, D)
                prev = jnp.concatenate([jnp.zeros_like(xb[:, :, :1]), xb[:, :, :-1]], axis=2)
                return jnp.concatenate([prev, xb], axis=3)
            kc, vc = (ctx(k), ctx(v))
            scores = jnp.einsum('bhnrd,bhncd->bhnrc', qb, kc)
            r = jnp.arange(Bk)[:, None]
            c = jnp.arange(2 * Bk)[None, :]
            band = (c >= r) & (c <= r + Bk)
            b_idx = jnp.arange(nb)[:, None, None]
            valid = band[None] & ((b_idx > 0) | (c[None] >= Bk))
            neg_inf = jnp.finfo(jnp.float32).min
            scores = jnp.where(valid[None, None], scores.astype(jnp.float32), neg_inf)
            attn = jax.nn.softmax(scores, axis=-1).astype(q.dtype)
            out = jnp.einsum('bhnrc,bhncd->bhnrd', attn, vc)
            return out.reshape(Bq, H, Tq, D)
        key = jax.random.key(seed)
        ks = jax.random.split(key, 11)
        f = jnp.float32
        return {'query': jax.random.normal(ks[0], (B, T, EMBED), f), 'key': jax.random.normal(ks[1], (B, T, EMBED), f), 'value': jax.random.normal(ks[2], (B, T, EMBED), f), 'wq': jax.random.normal(ks[3], (EMBED, EMBED), f) * 0.02, 'bq': jax.random.normal(ks[4], (EMBED,), f) * 0.02, 'wk': jax.random.normal(ks[5], (EMBED, EMBED), f) * 0.02, 'bk': jax.random.normal(ks[6], (EMBED,), f) * 0.02, 'wv': jax.random.normal(ks[7], (EMBED, EMBED), f) * 0.02, 'bv': jax.random.normal(ks[8], (EMBED,), f) * 0.02, 'wo': jax.random.normal(ks[9], (EMBED, EMBED), f) * 0.02, 'bo': jax.random.normal(ks[10], (EMBED,), f) * 0.02}
    _L0_xattn_all = _L0_xattn_setup()
    _L0_xattn_in = {k: v for k, v in _L0_xattn_all.items() if k in ('wq', 'bq', 'wk', 'bk', 'wv', 'bv', 'wo', 'bo')}
    del _L0_xattn_all

    def _L0_ffn_setup():
        import jax, jax.numpy as jnp
        import numpy as np
        E = 8
        K = 2
        D = 128
        H = 4 * D
        B, S = (4, 256)
        key = jax.random.key(seed)
        ks = jax.random.split(key, 6)
        scale = 0.02
        x = jax.random.normal(ks[0], (B, S, D), dtype=jnp.float32)
        Wr = jax.random.normal(ks[1], (D, E), dtype=jnp.float32) * scale
        br = jnp.zeros((E,), dtype=jnp.float32)
        Wg = jax.random.normal(ks[2], (E, D, H), dtype=jnp.float32) * scale
        Wu = jax.random.normal(ks[3], (E, D, H), dtype=jnp.float32) * scale
        Wd = jax.random.normal(ks[4], (E, H, D), dtype=jnp.float32) * scale
        return {'x': x, 'Wr': Wr, 'br': br, 'Wg': Wg, 'Wu': Wu, 'Wd': Wd}
    _L0_ffn_all = _L0_ffn_setup()
    _L0_ffn_in = {k: v for k, v in _L0_ffn_all.items() if k in ('Wr', 'br', 'Wg', 'Wu', 'Wd')}
    del _L0_ffn_all
    return {'x': x, 'ctx_1024': ctx_1024, 'g_xattn': g_xattn, 'g_ffn': g_ffn, 'L0_xattn_wq': _L0_xattn_in['wq'], 'L0_xattn_bq': _L0_xattn_in['bq'], 'L0_xattn_wk': _L0_xattn_in['wk'], 'L0_xattn_bk': _L0_xattn_in['bk'], 'L0_xattn_wv': _L0_xattn_in['wv'], 'L0_xattn_bv': _L0_xattn_in['bv'], 'L0_xattn_wo': _L0_xattn_in['wo'], 'L0_xattn_bo': _L0_xattn_in['bo'], 'L0_ffn_Wr': _L0_ffn_in['Wr'], 'L0_ffn_br': _L0_ffn_in['br'], 'L0_ffn_Wg': _L0_ffn_in['Wg'], 'L0_ffn_Wu': _L0_ffn_in['Wu'], 'L0_ffn_Wd': _L0_ffn_in['Wd']}

def reference(x, ctx_1024, g_xattn, g_ffn, L0_xattn_wq, L0_xattn_bq, L0_xattn_wk, L0_xattn_bk, L0_xattn_wv, L0_xattn_bv, L0_xattn_wo, L0_xattn_bo, L0_ffn_Wr, L0_ffn_br, L0_ffn_Wg, L0_ffn_Wu, L0_ffn_Wd):
    import jax
    import jax.numpy as jnp

    def _L0_xattn_ref(query, key, value, wq, bq, wk, bk, wv, bv, wo, bo):
        import jax, jax.numpy as jnp
        import numpy as np
        EMBED = 128
        HEADS = 16
        HEAD_DIM = EMBED // HEADS
        WINDOW = 128
        HALF = WINDOW // 2
        SCALE = HEAD_DIM ** (-0.5)
        B, T = (2, 512)

        def _sliding_window_attn(q, k, v):
            Bq, H, Tq, D = q.shape
            Bk = HALF
            nb = Tq // Bk
            qb = q.reshape(Bq, H, nb, Bk, D)

            def ctx(x):
                xb = x.reshape(Bq, H, nb, Bk, D)
                prev = jnp.concatenate([jnp.zeros_like(xb[:, :, :1]), xb[:, :, :-1]], axis=2)
                return jnp.concatenate([prev, xb], axis=3)
            kc, vc = (ctx(k), ctx(v))
            scores = jnp.einsum('bhnrd,bhncd->bhnrc', qb, kc)
            r = jnp.arange(Bk)[:, None]
            c = jnp.arange(2 * Bk)[None, :]
            band = (c >= r) & (c <= r + Bk)
            b_idx = jnp.arange(nb)[:, None, None]
            valid = band[None] & ((b_idx > 0) | (c[None] >= Bk))
            neg_inf = jnp.finfo(jnp.float32).min
            scores = jnp.where(valid[None, None], scores.astype(jnp.float32), neg_inf)
            attn = jax.nn.softmax(scores, axis=-1).astype(q.dtype)
            out = jnp.einsum('bhnrc,bhncd->bhnrd', attn, vc)
            return out.reshape(Bq, H, Tq, D)
        Bq, Tq, C = query.shape
        split = lambda x: x.reshape(Bq, Tq, HEADS, HEAD_DIM).transpose(0, 2, 1, 3)
        q = split(jnp.einsum('btc,oc->bto', query, wq) + bq) * SCALE
        k = split(jnp.einsum('btc,oc->bto', key, wk) + bk)
        v = split(jnp.einsum('btc,oc->bto', value, wv) + bv)
        o = _sliding_window_attn(q, k, v)
        o = o.transpose(0, 2, 1, 3).reshape(Bq, Tq, C)
        return jnp.einsum('btc,oc->bto', o, wo) + bo

    def _L0_ffn_ref(x, Wr, br, Wg, Wu, Wd):
        import jax, jax.numpy as jnp
        import numpy as np
        E = 8
        K = 2
        D = 128
        H = 4 * D
        B, S = (4, 256)
        router_logits = jnp.einsum('bsd,de->bse', x, Wr) + br
        topk_logits, topk_idx = jax.lax.top_k(router_logits, K)
        topk_w = jax.nn.softmax(topk_logits, axis=-1)
        gates = jnp.sum(jax.nn.one_hot(topk_idx, E, dtype=x.dtype) * topk_w[..., None], axis=-2)
        out = jnp.zeros_like(x)
        for e in range(E):
            h = jax.nn.silu(jnp.einsum('bsd,dh->bsh', x, Wg[e])) * jnp.einsum('bsd,dh->bsh', x, Wu[e])
            out = out + gates[..., e:e + 1] * jnp.einsum('bsh,hd->bsd', h, Wd[e])
        return out
    x = x + jnp.tanh(g_xattn[0]) * _L0_xattn_ref(_layernorm(x, axis=-1), ctx_1024, ctx_1024, L0_xattn_wq, L0_xattn_bq, L0_xattn_wk, L0_xattn_bk, L0_xattn_wv, L0_xattn_bv, L0_xattn_wo, L0_xattn_bo)
    x = x + jnp.tanh(g_ffn[0]) * _L0_ffn_ref(_layernorm(x, axis=-1), L0_ffn_Wr, L0_ffn_br, L0_ffn_Wg, L0_ffn_Wu, L0_ffn_Wd)
    return x

_drawn_inputs = setup_inputs


def setup_inputs(seed=0):
    import zlib

    import numpy as np

    out = dict(_drawn_inputs(seed))
    spreads = {'L0_ffn_br': (0.0, 0.8)}
    factors = {'L0_xattn_wq': 8.0,
     'L0_xattn_bq': 8.0,
     'L0_xattn_wk': 8.0,
     'L0_xattn_bk': 8.0,
     'L0_xattn_bv': 8.0,
     'L0_xattn_bo': 3.264,
     'L0_ffn_Wr': 8.0,
     'L0_ffn_Wg': 7.233,
     'L0_ffn_Wu': 7.197,
     'L0_ffn_Wd': 7.185}
    for name, (base, spread) in spreads.items():
        noise = np.random.default_rng([zlib.crc32(name.encode()), seed]).standard_normal(out[name].shape)
        drawn = base * np.exp(spread * noise) if base else spread * noise
        out[name] = jnp.asarray(drawn.astype(out[name].dtype))
    for name, factor in factors.items():
        out[name] = (out[name] * factor).astype(out[name].dtype)
    return out
```

```python
from contextlib import ExitStack, contextmanager

import concourse.bass as bass
from concourse import mybir

ALU = mybir.AluOpType
ACT = mybir.ActivationFunctionType
AX = mybir.AxisListType
F32 = mybir.dt.float32
F16 = mybir.dt.float16
BF16 = mybir.dt.bfloat16
I32 = mybir.dt.int32

P = 128
NEG = -1.0e30
EPS = 1.0e-5


class LoopChain:

    def __init__(self, eng, chain, steps, turns):
        self.eng, self.chain, self.steps, self.turns = eng, chain, steps, turns

    @contextmanager
    def Fori(self, start, end):
        with self.eng.Fori(start, end) as i:
            self.chain.turn(i - start, self.steps)
            yield i
        self.chain.end(self.turns)


class Chain:

    def __init__(self, eng, sem):
        self.eng, self.sem, self.base, self.n, self.steps = eng, sem, 0, 0, 0

    def __call__(self, instruction):
        instruction.then_inc(self.sem, 1)
        self.n += 1
        self.eng.wait_ge(self.sem, self.base + self.n)

    def turn(self, i, steps):
        self.start, self.steps = self.n, steps
        self.base = i * steps

    def end(self, turns):
        assert self.n - self.start == self.steps, (self.n - self.start, self.steps)
        self.base, self.n = 0, self.start + self.steps * turns


def flamingo_gated_block(nc, x, ctx_in, g_xattn, g_ffn, wq, bq, wk, bk, wv, bv, wo, bo, Wr, br, Wg, Wu, Wd, out):
    B, T, D = x.shape
    E, _, H = Wg.shape
    HEADS = 16
    HD = D // HEADS
    SCALE = HD ** -0.5
    N = B * T
    NT = N // P
    NQ = NT // 4
    CH = 2 * P
    NCH = N // CH
    HC = H // P
    K = 2
    FT = (N * K) // P + E - 1
    TRASH = E * N
    XROWS = TRASH + (FT - N * K // P) * P
    R6 = 6
    XW = 2 * D + 2
    assert (T, D, HD, HC, NQ, NCH, FT) == (64, P, 8, 4, 4, 8, 39)

    x_t = x.rearrange("(t b) q c -> (b q) t c", b=2)
    c_t = ctx_in.rearrange("(t b) q c -> (b q) t c", b=2)
    out_t = out.rearrange("(t b) q c -> (b q) t c", b=2)

    with ExitStack() as ctx:
        def sb(name, shape, dt):
            return ctx.enter_context(nc.sbuf_tensor(name, shape, dt))

        def sem(name):
            return ctx.enter_context(nc.semaphore(name))

        def dram(name, shape, dt):
            return nc.dram_tensor(name, shape, dt, kind="Internal").ap()

        q_parts = dram("q_parts", [3, HD, HEADS, N], F16)
        k_parts = dram("k_parts", [3, HD, HEADS, N], F16)
        routed = dram("routed", [XROWS, XW], F16)
        expert_out = dram("expert_out", [N * K, D], F32)

        X = sb("X", [P, NT, D], F32)
        C = sb("C", [P, NT, D], F32)
        XN = sb("XN", [P, 2, 4, D], F32)
        xT = sb("xT", [P, 2, 512], F32)
        cT = sb("cT", [P, 2, 512], F32)
        QK = sb("QK", [P, 2, 2, 2, 512], F16)
        w_nat = sb("w_nat", [P, 4, D], F32)
        wqT = sb("wqT", [P, D], F32)
        wkT = sb("wkT", [P, D], F32)
        wvT = sb("wvT", [P, D], F32)
        woT = sb("woT", [P, D], F32)
        woP = sb("woP", [P, 2, P], F32)
        WO = sb("WO", [P, 2, D], F32)
        bq_c = sb("bq_c", [P, 1], F32)
        bqs_c = sb("bqs_c", [P, 1], F32)
        bk_c = sb("bk_c", [P, 1], F32)
        bv_c = sb("bv_c", [P, 1], F32)
        bvb = sb("bvb", [P, P], F32)
        bo_b = sb("bo_b", [P, D], F32)
        bias_row = sb("bias_row", [P, D], F32)
        br_b = sb("br_b", [P, E], F32)
        wr_sb = sb("wr_sb", [P, E], F32)
        gx = sb("gx", [P, 2], F32)
        tg = sb("tg", [P, 2], F32)
        ident = sb("ident", [P, P], F32)
        ident16 = sb("ident16", [P, P], F16)
        identb = sb("identb", [P, P], BF16)
        ones_f = sb("ones_f", [P, P], F32)
        mask_q = sb("mask_q", [P, 64], BF16)
        shift_w = sb("shift_w", [96, 16, P], BF16)
        shift_m = sb("shift_m", [96, 2, P], BF16)
        before = sb("before", [P, P], BF16)
        ones_b = sb("ones_b", [P, P], BF16)
        QE = sb("QE", [P, 2, 4, 4, CH], F16)
        KS = sb("KS", [P, 2, 4, CH], F16)
        VB = sb("VB", [P, NT, HEADS, 36], F16)
        VR = sb("VR", [P, 2, HEADS * 36], F16)
        VRw = VR[:, :, :].rearrange("p a n -> p (a n)").bitcast(F32).rearrange("p (a n) -> p a n", a=2)
        VBw = VB[:, :, :, :].rearrange("p t h w -> p (t h w)").bitcast(F32)
        MX = sb("MX", [P, 2, 8, 4], F32)
        P32 = sb("P32", [P, 2, 512], F32)
        PH = sb("PH", [P, 2, 1024], F16)
        PL = sb("PL", [P, 2, 1024], F16)
        SM = sb("SM", [P, 8, 18], F32)
        RS = sb("RS", [P, 8, 2], F32)
        O = sb("O", [P, NT, D], F32)
        stats = sb("stats", [P, 4, 6], F32)
        mv = sb("mv", [P, 4, 2], F32)
        ve = sb("ve", [P, 4], F32)
        lnv = sb("lnv", [P, 4], F32)
        r0 = sb("r0", [P, 4], F32)
        nt = sb("nt", [P, 4], F32)
        X2 = C
        OT = xT
        XN2T = cT
        ids = sb("ids", [P, NT, K], I32)
        XHL = sb("XHL", [P, 2, K, 4, XW], F16)
        lg = sb("lg", [P, 4, E], F32)
        le = sb("le", [P, 4, E], F32)
        tie = sb("tie", [P, E], F32)
        ebase = sb("ebase", [P, E], F32)
        m1 = sb("m1", [P, 4], F32)
        m2 = sb("m2", [P, 4], F32)
        tm = sb("tm", [P, 4], F32)
        oh1 = sb("oh1", [P, 4, E], F32)
        oh2 = sb("oh2", [P, 4, E], F32)
        oh1b = sb("oh1b", [P, 4, E], F32)
        oh2b = sb("oh2b", [P, 4, E], F32)
        ohb = sb("ohb", [P, 4, E], BF16)
        rank = sb("rank", [P, 4, E], F32)
        posf = sb("posf", [P, K, 4], F32)
        pos = sb("pos", [P, 2, K, 4], I32)
        runs = sb("runs", [P, E], F32)
        gw = sb("gw", [P, NT, K], F32)
        cnt_i = sb("cnt_i", [1, E], I32)
        cnt_f = sb("cnt_f", [1, E], F32)
        tiles_to = sb("tiles_to", [1, E], F32)
        eint = sb("eint", [P, E], I32)
        jint = sb("jint", [1, FT], I32)
        jrow = sb("jrow", [1, FT], F32)
        jge = sb("jge", [1, FT, E], F32)
        jex = sb("jex", [1, FT], F32)
        jbk = sb("jbk", [1, FT], F32)
        tile_row = sb("tile_row", [1, FT + 1], I32)
        tile_exp = sb("tile_exp", [1, FT + 1], I32)
        fill = sb("fill", [P, 5, XW], F16)
        WS = sb("WS", [P, 2, 3, 512], F32)
        WG = sb("WG", [P, E * 2048], F16)
        WD = sb("WD", [P, E * HC * 256], F16)

        XG = sb("XG", [P, R6, XW], F16)
        XGT = sb("XGT", [P, 2, 2, P], F16)
        YT = sb("YT", [P, D], F32)
        QEf = QE[:, :, :, :, :].rearrange("p a r g t -> p (a r g t)").bitcast(F32)
        SG = QEf[:, 0:2 * H].rearrange("p (a n) -> p a n", a=2)
        HF = QEf[:, 2 * H:4 * H].rearrange("p (a n) -> p a n", a=2)
        HH = sb("HH", [P, 2, 2, H], F16)
        HT = sb("HT", [P, 2, 2, H], F16)
        YS = sb("YS", [P, R6, D], F32)
        YA = O
        bank = [ctx.enter_context(nc.psum_tensor(f"bank{i}", [P, 512], F32)) for i in range(8)]

        WGv = WG[:, :].rearrange("p (e k n) -> p e k n", e=E, k=4)
        WDv = WD[:, :].rearrange("p (e h k n) -> p e h k n", e=E, h=HC, k=2)
        parts_q = q_parts.rearrange("c d (g r) t -> r (c d) g t", r=4)
        parts_k = k_parts.rearrange("c d (g r) t -> r (c d) g t", r=4)

        s_weights = sem("s_weights")
        s_x = [sem("s_x0"), sem("s_x1")]
        s_pool = sem("s_pool")
        s_turns = sem("s_turns")
        s_yt = sem("s_yt")
        s_consts = sem("s_consts")
        s_dconsts = sem("s_dconsts")
        s_fill = sem("s_fill")
        s_wt = sem("s_wt")
        s_wev = sem("s_wev")
        s_wperm = sem("s_wperm")
        s_tanh = sem("s_tanh")
        s_bias = sem("s_bias")
        s_dve = sem("s_dve")
        s_act = sem("s_act")
        s_var = sem("s_var")
        s_rs = sem("s_rs")
        s_xn = sem("s_xn")
        s_tr = sem("s_tr")
        s_trev = sem("s_trev")
        s_qkv = sem("s_qkv")
        s_hi = sem("s_hi")
        s_lo = sem("s_lo")
        s_parts = [sem("s_parts0"), sem("s_parts1")]
        s_stack = [sem("s_stack0"), sem("s_stack1")]
        s_sc = sem("s_sc")
        s_max = sem("s_max")
        s_mt = sem("s_mt")
        s_shift = sem("s_shift")
        s_st = sem("s_st")
        s_exp = sem("s_exp")
        s_vr = sem("s_vr")
        s_ph = sem("s_ph")
        s_pl = sem("s_pl")
        s_pv = sem("s_pv")
        s_o = sem("s_o")
        s_ws = [sem("s_ws0"), sem("s_ws1")]
        s_wh = sem("s_wh")
        s_wl = sem("s_wl")
        s_ot = sem("s_ot")
        s_otev = sem("s_otev")
        s_op = sem("s_op")
        s_x2 = sem("s_x2")
        s_rv = sem("s_rv")
        s_rrs = sem("s_rrs")
        s_xn2 = sem("s_xn2")
        s_x2t = sem("s_x2t")
        s_x2ev = sem("s_x2ev")
        s_lg = sem("s_lg")
        s_gexp = sem("s_gexp")
        s_gin = sem("s_gin")
        s_oh = sem("s_oh")
        s_rk = sem("s_rk")
        s_pos = sem("s_pos")
        s_sent = [sem("s_sent0"), sem("s_sent1")]
        s_table = sem("s_table")
        s_xg = [sem(f"s_xg{i}") for i in range(R6)]
        s_xt = sem("s_xt")
        s_xtev = sem("s_xtev")
        s_gu = sem("s_gu")
        s_silu = sem("s_silu")
        s_h = sem("s_h")
        s_hh = sem("s_hh")
        s_hl = sem("s_hl")
        s_ht = sem("s_ht")
        s_htev = sem("s_htev")
        s_y = sem("s_y")
        s_yev = sem("s_yev")
        s_ysent = [sem(f"s_ysent{i}") for i in range(R6)]
        s_ya = [sem(f"s_ya{i}") for i in range(4)]
        s_fin = sem("s_fin")
        s_out = sem("s_out")

        N_CONST = 15
        N_W = 4 + 2 * HD + 6
        block = ctx.enter_context(nc.Block())

        def experts(eng, ffn_step, turns=None):
            ffn_step(0, 0, True, False, False)
            ffn_step(1, 1, True, True, False)
            with eng.Fori(0, 6) as i:
                for u in range(2, 2 + R6):
                    if turns is not None:
                        turns[0], turns[1] = i + 1, i + 2
                    ffn_step(R6 * i + u, u, True, True, True)
            if turns is not None:
                turns[0], turns[1] = 7, 8
            ffn_step(FT - 1, 2, "last", True, True)
            ffn_step(FT, 3, False, True, True)
            ffn_step(FT + 1, 4, False, False, True)

        def attention(eng, lead, follow, last):
            lead(0, 0, 0, True)
            lead(1, 1, 0, False)
            follow(0, 0, 0, True)
            lead(2, 0, 1, False)
            follow(1, 1, 0, False)
            with eng.Fori(1, 3) as i:
                lead(2 * i + 1, 1, i, False)
                follow(2 * i, 0, i, False)
                lead(2 * i + 2, 0, i + 1, False)
                follow(2 * i + 1, 1, i, False)
            lead(NCH - 1, 1, 3, False)
            follow(NCH - 2, 0, 3, False)
            last()
            follow(NCH - 1, 1, 3, False)

        YAf = [O[:, 8 * i:8 * i + 8, :] for i in (0, 1)]
        YAq = [v.rearrange("p (t k) n -> p t (k n)", k=K) for v in YAf]
        YAk = [v.rearrange("p (t k) n -> p t k n", k=K) for v in YAf]

        @block.sync
        def _(sp):
            for t in range(NQ):
                if t >= 2:
                    sp.wait_ge(s_x[t % 2], 32)
                sp.dma_start(X[:, 4 * t:4 * t + 4, :], x_t[:, 4 * t:4 * t + 4, :]).then_inc(s_x[t % 2], 16)
                sp.dma_start(C[:, 4 * t:4 * t + 4, :], c_t[:, 4 * t:4 * t + 4, :]).then_inc(s_x[t % 2], 16)
                if t == 0:
                    for n, w in enumerate((wq, wk, wv, wo)):
                        sp.dma_start(w_nat[:, n, :], w).then_inc(s_weights, 16)
                    for b_dram, b_sb in ((bq, bq_c), (bk, bk_c)):
                        by_d = b_dram.rearrange("(h d o) -> d h o", d=HD, o=1)
                        for d in range(HD):
                            sp.dma_start(b_sb[HEADS * d:HEADS * (d + 1), :], by_d[d],
                                         allow_slow_non_contiguous=True).then_inc(s_weights, 16)
                    sp.dma_start(bv_c[:, :], bv.rearrange("(p o) -> p o", o=1)).then_inc(s_weights, 16)
                    sp.dma_start(bo_b[:, :], bo.partition_broadcast(P)).then_inc(s_weights, 16)
                    sp.dma_start(br_b[:, :], br.partition_broadcast(P)).then_inc(s_weights, 16)
                    sp.dma_start(wr_sb[:, :], Wr).then_inc(s_weights, 16)
                    sp.dma_start(gx[:, 0:1], g_xattn.partition_broadcast(P)).then_inc(s_weights, 16)
                    sp.dma_start(gx[:, 1:2], g_ffn.partition_broadcast(P)).then_inc(s_weights, 16)

            def write_parts(t, par):
                sp.wait_ge(s_lo, 3 * t + 2)
                for n, (parts, order) in enumerate(((q_parts, (0, 0, 1)), (k_parts, (0, 1, 0)))):
                    for c, half in enumerate(order):
                        sp.dma_start(parts[c].rearrange("d h t -> (d h) t")[:, bass.ds(t * 512, 512)],
                                     QK[:, par, n, half, :]).then_inc(s_parts[par], 16)

            def load_stack(c, par, k):
                sp.wait_ge(s_st, 4 * c + 4)
                for r in range(4):
                    sp.dma_start(QE[32 * r:32 * r + 24, par, r, :, :],
                                 parts_q[r][:, :, bass.ds(c * CH, CH)]).then_inc(s_stack[par], 16)
                    sp.dma_start(KS[32 * r:32 * r + 24, par, :, :],
                                 parts_k[r][:, :, bass.ds(c * CH, CH)]).then_inc(s_stack[par], 16)

            def load_expert(e, par):
                sp.wait_ge(s_wl, e + 1)
                sp.dma_start(WS[:, par, 0, :], Wg[bass.ds(e, 1)].rearrange("o d h -> (o d) h")).then_inc(s_ws[par], 16)
                sp.dma_start(WS[:, par, 1, :], Wu[bass.ds(e, 1)].rearrange("o d h -> (o d) h")).then_inc(s_ws[par], 16)
                sp.dma_start(WS[:, par, 2, :].rearrange("p (c n) -> p c n", c=HC),
                             Wd[bass.ds(e, 1)].rearrange("o (c p) n -> p (o c) n", p=P)).then_inc(s_ws[par], 16)

            sp.wait_ge(s_dconsts, 2)
            write_parts(0, 0)
            sp.wait_ge(s_parts[0], 96)
            load_stack(0, 0, 0)
            load_stack(1, 1, 0)
            write_parts(1, 1)
            write_parts(2, 0)
            write_parts(3, 1)
            load_expert(0, 0)
            load_expert(1, 1)
            sp.wait_ge(s_consts, N_CONST)
            r_fill = routed.rearrange("(n p m) w -> n p (m w)", p=P, m=5)
            for n in range(r_fill.shape[0]):
                sp.dma_start(r_fill[n], fill[:, :, :].rearrange("p m w -> p (m w)")).then_inc(s_fill, 16)
            for p_ in (0, 1):
                sp.wait_ge(s_parts[p_], 2 * 96)
            with sp.Fori(1, NCH // 2) as i:
                for par in (0, 1):
                    load_stack(2 * i + par, par, i)
                    load_expert(2 * i + par, par)

            sp.wait_ge(s_fill, 16 * r_fill.shape[0])
            sp.wait_ge(s_sent[0], 2 * 8 * 16)
            sp.wait_ge(s_sent[1], 2 * 8 * 16)
            sp.wait_ge(s_table, 2)

            def load_rows(j, u):
                row = sp.value_load(tile_row[0:1, bass.ds(j, 1)], min_val=0, max_val=XROWS - P)
                sp.dma_start(XG[:, u, :], routed[bass.ds(row, P), :]).then_inc(s_xg[u], 16)

            for j in range(R6):
                load_rows(j, j)
            with sp.Fori(1, 6) as i:
                for u in range(R6):
                    sp.wait_ge(s_ysent[u], i * 16)
                    load_rows(R6 * i + u, u)
            for u in range(FT - 6 * R6):
                sp.wait_ge(s_ysent[u], 6 * 16)
                load_rows(6 * R6 + u, u)
            for u in range(R6):
                sp.wait_ge(s_ysent[u], 16 * (7 if u < FT - 6 * R6 else 6))
            r_out = expert_out[0:N * K, :].rearrange("(t p k) n -> p t (k n)", p=P, k=K)
            for q in range(NQ):
                if q >= 2:
                    sp.wait_ge(s_fin, q - 1)
                sp.dma_start(YAq[q % 2], r_out[:, 4 * q:4 * q + 4, :]).then_inc(s_ya[q], 16)
            for q in range(NQ):
                sp.wait_ge(s_fin, q + 1)
                sp.dma_start(out_t[:, 4 * q:4 * q + 4, :], X2[:, 4 * q:4 * q + 4, :]).then_inc(s_out, 16)
            sp.wait_ge(s_out, 16 * NQ)


        @block.gpsimd
        def _(pool):
            pool.memset(ident[:, :], 0.0)
            pool.memset(ident16[:, :], 0.0)
            pool.memset(identb[:, :], 0.0)
            pool.memset(mask_q[:, :], 0.0)
            pool.memset(shift_w[:, :, :], 0.0)
            pool.memset(shift_m[:, :, :], 0.0)
            pool.memset(before[:, :], 1.0)
            pool.memset(ones_b[:, :], 1.0)
            pool.memset(VB[:, :, :, :].rearrange("p t h w -> p (t h w)").bitcast(F32), 0.0)
            pool.memset(fill[:, :, :].rearrange("p m w -> p (m w)").bitcast(F32), 0.0).then_inc(s_pool, 1)
            pool.wait_ge(s_pool, 1)
            const = Chain(pool, s_consts)
            for t in (ident, ident16, identb):
                const(pool.affine_select(out=t[:, :], in_=t[:, :], compare_op=ALU.not_equal, fill=1.0,
                                   base=0, pattern=[[-1, P]], channel_multiplier=1))
            for r in (0, 1):
                m = mask_q[64 * r:64 * r + 64, :]
                const(pool.affine_select(out=m, in_=m, compare_op=ALU.is_ge, fill=NEG,
                                   base=0, pattern=[[-1, 64]], channel_multiplier=1))
            m = shift_w[0:64, :, :].rearrange("p v (b k) -> p (v b) k", b=2)
            const(pool.affine_select(out=m, in_=m, compare_op=ALU.is_ge, fill=NEG,
                               base=0, pattern=[[0, 32], [-1, 64]], channel_multiplier=1))
            m = shift_w[64:96, :, :].rearrange("p v (b k) -> p v b k", b=2)
            const(pool.affine_select(out=m, in_=m, compare_op=ALU.not_equal, fill=1.0,
                               base=0, pattern=[[-2, 16], [-1, 2], [0, 64]], channel_multiplier=1))
            m = shift_m[0:64, :, :].rearrange("p a (b k) -> p (a b) k", b=2)
            const(pool.affine_select(out=m, in_=m, compare_op=ALU.not_equal, fill=1.0,
                               base=0, pattern=[[0, 4], [-1, 64]], channel_multiplier=1))
            const(pool.affine_select(out=before[:, :], in_=before[:, :], compare_op=ALU.is_gt, fill=0.0,
                               base=0, pattern=[[1, P]], channel_multiplier=-1))
            const(pool.memset(VB[0:64, :, :, 8:9], 1.0))
            const(pool.memset(VB[64:P, :, :, 17:18], 1.0))
            const(pool.iota(ids[:, :, :], pattern=[[2 * P, NT], [1, K]], channel_multiplier=2))
            const(pool.iota(eint[:, :], pattern=[[1, E]], channel_multiplier=0))
            const(pool.iota(jint[:, :], pattern=[[1, FT]], channel_multiplier=0))
            const(pool.memset(fill[:, :, 2 * D:XW].bitcast(I32), N * K))

            def low_halves(e, par):
                g_hi, u_lo = WG[:, bass.ds(e * 2048, 1024)], WG[:, bass.ds(e * 2048 + 1024, 1024)]
                pool.wait_ge(s_wh, 2 * e + 1)
                pool.tensor_tensor(u_lo, WS[:, par, 0:2, :].rearrange("p k n -> p (k n)"), g_hi, ALU.subtract)
                pool.wait_ge(s_wh, 2 * e + 2)
                pool.tensor_tensor(WDv[:, bass.ds(e, 1), :, 1, :].rearrange("p o h n -> p (o h) n"),
                                   WS[:, par, 2, :].rearrange("p (h n) -> p h n", h=HC),
                                   WDv[:, bass.ds(e, 1), :, 0, :].rearrange("p o h n -> p (o h) n"),
                                   ALU.subtract).then_inc(s_wl, 1)

            def lead(c, par, k, first):
                for tt in (0, 1):
                    pool.wait_ge(s_pv, 2 * c + tt + 1)
                    pool.tensor_copy(VRw[:, tt, :], VBw[:, bass.ds((2 * c + tt) * 288, 288)]).then_inc(s_vr, 1)

            pool.wait_ge(s_lo, 3 * NQ)
            attention(pool, lead, lambda c, par, k, first: low_halves(c, par), lambda: None)

            pool.wait_ge(s_fill, 16 * 27)
            for q in range(NQ):
                par = q % 2
                pool.wait_ge(s_pos, q + 1)
                for k in range(K):
                    for j in range(4):
                        pool.indirect_dma_start(
                            out=routed[:, :], out_offset=bass.IndirectOffsetOnAxis(ap=pos[:, par, k, j:j + 1], axis=0),
                            in_=XHL[:, par, k, j, :], in_offset=None).then_inc(s_sent[par], 16)

            last_row = pool.to_reg(N * K - 1)

            def scatter(j, u):
                pool.wait_ge(s_table, 2)
                pool.wait_ge(s_yev, j + 1)
                pool.sem_inc(s_turns, 1)
                pool.indirect_dma_start(
                    out=expert_out[:, :],
                    out_offset=bass.IndirectOffsetOnAxis(ap=XG[:, u, 2 * D:XW].bitcast(I32), axis=0),
                    in_=YS[:, u, :], in_offset=None,
                    bounds_check=last_row, oob_is_err=False).then_inc(s_ysent[u], 16)

            with pool.Fori(0, 6) as i:
                for u in range(R6):
                    scatter(R6 * i + u, u)
            for u in range(FT - 6 * R6):
                scatter(6 * R6 + u, u)

        @block.scalar
        def _(act):
            step = Chain(act, s_act)

            act.wait_ge(s_wt, 1)
            act.activation(wqT[:, :].rearrange("c (d h) -> c h d", d=HD),
                           bank[0][:, 0:P].rearrange("c (h d) -> c h d", d=HD), ACT.Copy, scale=SCALE).then_inc(s_wev, 1)
            act.activation(wkT[:, :].rearrange("c (d h) -> c h d", d=HD),
                           bank[1][:, 0:P].rearrange("c (h d) -> c h d", d=HD), ACT.Copy).then_inc(s_wev, 1)
            act.activation(wvT[:, :], bank[2][:, 0:P], ACT.Copy).then_inc(s_wev, 1)
            act.activation(woT[:, :], bank[3][:, 0:P], ACT.Copy).then_inc(s_wev, 1)
            act.wait_ge(s_wt, 2)
            for r in (0, 1):
                act.activation(WO[:, r, :], bank[4][:, r * P:r * P + P], ACT.Copy).then_inc(s_wev, 1)
            act.wait_ge(s_weights, 16 * N_W)
            act.activation(tg[:, :], gx[:, :], ACT.Tanh).then_inc(s_tanh, 1)

            def rsqrt(v_ready, n, done):
                act.wait_ge(v_ready, n)
                step(act.activation(lnv[:, :], ve[:, :], ACT.Ln))
                act.activation(r0[:, :], lnv[:, :], ACT.Exp, scale=-0.5).then_inc(done, 1)

            rsqrt(s_var, 1, s_rs)
            rsqrt(s_var, 2, s_rs)
            for t in range(NQ):
                par = t % 2
                act.wait_ge(s_tr, 2 * t + 1)
                act.activation(xT[:, par, :], bank[0][:, :], ACT.Copy).then_inc(s_trev, 1)
                act.wait_ge(s_tr, 2 * t + 2)
                act.activation(cT[:, par, :], bank[1][:, :], ACT.Copy).then_inc(s_trev, 1)
                if t >= 2:
                    act.wait_ge(s_parts[par], 96)
                act.wait_ge(s_qkv, 3 * t + 1)
                act.activation(QK[:, par, 0, 0, :], bank[2 + par][:, :], ACT.Identity, bias=bqs_c[:, 0:1]).then_inc(s_hi, 1)
                act.wait_ge(s_qkv, 3 * t + 2)
                act.activation(QK[:, par, 1, 0, :], bank[4 + par][:, :], ACT.Identity, bias=bk_c[:, 0:1]).then_inc(s_hi, 1)
                act.wait_ge(s_qkv, 3 * t + 3)
                for b in (0, 1):
                    rows = slice(64 * b, 64 * b + 64)
                    v = act.activation(VB[rows, 4 * t:4 * t + 4, :, 9 * b:9 * b + 8],
                                       bank[6 + par][rows, :].rearrange("p (t h d) -> p t h d", t=4, d=HD), ACT.Copy)
                v.then_inc(s_hi, 1)
                if t + 2 < NQ:
                    rsqrt(s_var, t + 3, s_rs)

            def lead(c, par, k, first):
                pass

            def follow(c, par, k, first):
                act.wait_ge(s_mt, c + 3)
                act.wait_ge(s_st, 4 * c + 4)
                act.activation(shift_m[64:96, par, :], bank[6][0:32, 0:P], ACT.Copy, scale=-1.0).then_inc(s_shift, 1)
                for tt in (0, 1):
                    for gp in (0, 1):
                        m = 4 * c + 2 * tt + gp
                        act.wait_ge(s_st, m + 9)
                        act.wait_ge(s_pl, m + 1)
                        act.activation(P32[:, gp, :], bank[2 + gp][:, :], ACT.Exp).then_inc(s_exp, 1)
                        if gp == 0:
                            act.wait_ge(s_pv, 2 * c + tt + 1)
                        act.wait_ge(s_exp, m + 3)
                        act.activation(PH[:, tt, 512 * gp:512 * gp + 512], P32[:, gp, :], ACT.Copy).then_inc(s_ph, 1)
                act.wait_ge(s_ws[par], 48 * (k + 1))
                act.activation(WG[:, bass.ds(c * 2048, 1024)],
                               WS[:, par, 0:2, :].rearrange("p k n -> p (k n)"), ACT.Copy).then_inc(s_wh, 1)
                act.activation(WDv[:, bass.ds(c, 1), :, 0, :].rearrange("p o h n -> p (o h) n"),
                               WS[:, par, 2, :].rearrange("p (h n) -> p h n", h=HC), ACT.Copy).then_inc(s_wh, 1)

            attention(act, lead, follow, lambda: None)

            for s in range(NQ + 1):
                if s < NQ:
                    act.wait_ge(s_ot, s + 1)
                    if s >= 2:
                        act.wait_ge(s_op, s - 1)
                    act.activation(OT[:, s % 2, :], bank[0][:, :], ACT.Copy).then_inc(s_otev, 1)
                    rsqrt(s_rv, s + 1, s_rrs)
                if s >= 1:
                    q = s - 1
                    act.wait_ge(s_x2t, q + 1)
                    act.activation(XN2T[:, q % 2, :], bank[2][:, :], ACT.Copy).then_inc(s_x2ev, 1)
                    act.wait_ge(s_gin, q + 1)
                    act.activation(m2[:, :], m2[:, :], ACT.Exp).then_inc(s_gexp, 1)

            def silu(s, p):
                act.wait_ge(s_gu, s + 1)
                act.activation(SG[:, p, :], bank[p][:, :], ACT.Silu).then_inc(s_silu, 1)

            def high(s, p):
                act.wait_ge(s_h, s + 3)
                act.wait_ge(s_ht, s + 1)
                act.activation(HH[:, p, 0, :], HF[:, p, :], ACT.Copy).then_inc(s_hh, 1)

            def hidden_out(s, p):
                act.wait_ge(s_ht, s + 3)
                act.wait_ge(s_y, s + 1)
                act.activation(HT[:, p, :, :].rearrange("p k n -> p (k n)"), bank[4 + p][:, :].bitcast(F16), ACT.Copy)\
                   .then_inc(s_htev, 1)

            def ffn_step(s, u, gu, th, dn):
                if gu:
                    silu(s, u % 2)
                    high(s, u % 2)
                if th:
                    hidden_out(s - 1, (u + 1) % 2)

            experts(act, ffn_step)

        @block.tensor
        def _(pe):
            def mm(o, a, b, start, stop=False):
                return pe.matmul(o, a, b, start=start, stop=stop, skip_group_check=True)

            pe.wait_ge(s_consts, N_CONST)
            pe.wait_ge(s_weights, 16 * N_W)
            for n in range(4):
                tr = pe.transpose(bank[n][:, 0:P], w_nat[:, n, :], ident[:, :])
            tr.then_inc(s_wt, 1)
            pe.wait_ge(s_wperm, 1)
            for r in (0, 1):
                tr = pe.transpose(bank[4][:, r * P:r * P + P], woP[:, r, :], ident[:, :])
            tr.then_inc(s_wt, 1)
            pe.wait_ge(s_wev, 4)
            pe.wait_ge(s_wperm, 2)
            mm(bank[5][:, 0:P], bvb[:, :], woT[:, :], True, True).then_inc(s_wt, 1)
            pe.wait_ge(s_wev, 6)
            pe.wait_ge(s_bias, 1)

            for t in range(NQ):
                par = t % 2
                pe.wait_ge(s_xn, t + 1)
                pe.wait_ge(s_trev, 2 * t)
                for j in range(4):
                    tr = pe.transpose(bank[0][:, P * j:P * j + P], XN[:, par, j, :], ident[:, :])
                tr.then_inc(s_tr, 1)
                pe.wait_ge(s_x[par], 32 * (t // 2 + 1))
                for j in range(4):
                    tr = pe.transpose(bank[1][:, P * j:P * j + P], C[:, 4 * t + j, :], ident[:, :])
                tr.then_inc(s_tr, 1)
                if t >= 2:
                    pe.wait_ge(s_lo, 3 * (t - 1))
                pe.wait_ge(s_trev, 2 * t + 1)
                mm(bank[2 + par][:, :], wqT[:, :], xT[:, par, :], True, True).then_inc(s_qkv, 1)
                pe.wait_ge(s_trev, 2 * t + 2)
                mm(bank[4 + par][:, :], wkT[:, :], cT[:, par, :], True, True).then_inc(s_qkv, 1)
                for j in range(4):
                    v = mm(bank[6 + par][:, P * j:P * j + P], cT[:, par, P * j:P * j + P], wvT[:, :], j == 0, True)
                v.then_inc(s_qkv, 1)
            pe.wait_ge(s_lo, 3 * NQ)

            def max_rows(c, par):
                pe.wait_ge(s_max, 4 * c + 6)
                pe.wait_ge(s_shift, c)
                pe.transpose(bank[6][0:32, 0:P], MX[:, par, :, :].rearrange("p v t -> p (v t)"), ident[:, :])\
                  .then_inc(s_mt, 1)

            def lead(c, par, k, first):
                pe.wait_ge(s_stack[par], 128 * (k + 1))
                for tt in (0, 1):
                    for b in (0, 1):
                        toks = slice(P * tt + 64 * b, P * tt + 64 * b + 64)
                        pe.wait_ge(s_max, 4 * c + 2 * tt + b + 1)
                        mm(bank[b][:, :], identb[:, :], mask_q[:, :].unsqueeze(1).to_broadcast([P, 8, 64]), True)
                        for rp in (0, 1):
                            for g in range(4):
                                at = 64 * (4 * rp + g)
                                for r in (0, 1):
                                    sc = mm(bank[b][64 * r:64 * r + 64, at:at + 64], QE[:, par, 2 * rp + r, g, toks],
                                            KS[:, par, g, toks], False, True)
                        sc.then_inc(s_sc, 1)
                    if tt == 0 and not first:
                        max_rows(c - 1, 1 - par)

            def products(t, tpar):
                pe.wait_ge(s_vr, t + 1)
                pe.wait_ge(s_ph, 2 * t + 2)
                pe.wait_ge(s_pl, 2 * t + 4)
                pe.wait_ge(s_o, t + 1)
                for g in range(4):
                    for r in range(4):
                        r1, at = 64 * (r % 2), 36 * (2 * g + r // 2)
                        col, at_v = 256 * g + 64 * r, 36 * (4 * g + r)
                        mm(bank[4 + tpar][r1:r1 + 64, at:at + 36], PH[:, tpar, col:col + 64], VR[:, tpar, at_v:at_v + 36],
                           g == 0 and r < 2)
                        pv = mm(bank[4 + tpar][r1:r1 + 64, at:at + 18], PL[:, tpar, col:col + 64], VR[:, tpar, at_v:at_v + 18], False, True)
                pv.then_inc(s_pv, 1)

            def follow(c, par, k, first):
                pe.wait_ge(s_shift, c + 1)
                for tt in (0, 1):
                    for gp in (0, 1):
                        pe.wait_ge(s_exp, 4 * c + 2 * tt + gp + 1)
                        for g2 in (0, 1):
                            for rp in (0, 1):
                                at = 256 * g2 + 128 * rp
                                mm(bank[2 + gp][:, at:at + P], shift_w[:, (4 * rp + 2 * gp + g2) * 2 + tt, :],
                                   shift_m[:, par, :], g2 == 0 and rp == 0)
                        for g2 in (0, 1):
                            for b in (0, 1):
                                toks = slice(P * tt + 64 * b, P * tt + 64 * b + 64)
                                st = mm(bank[2 + gp][64 * b:64 * b + 64, 256 * g2:256 * g2 + 256],
                                        KS[:, par, 2 * gp + g2, toks], QE[:, par, :, 2 * gp + g2, toks], False, True)
                        st.then_inc(s_st, 1)
                    if not (first and tt == 0):
                        products(2 * c + tt - 1, 1 - tt)

            attention(pe, lead, follow, lambda: max_rows(NCH - 1, 1))
            products(NT - 1, 1)

            pe.wait_ge(s_o, NT + 2)
            for s in range(NQ + 2):
                if s >= 2:
                    q = s - 2
                    pe.wait_ge(s_oh, q + 1)
                    pe.wait_ge(s_pos, q)
                    oh = ohb[:, :, :].rearrange("p t e -> p (t e)")
                    mm(bank[4][:, 0:4 * E], before[:, :], oh, True, True)
                    mm(bank[4][:, 4 * E:8 * E], ones_b[:, :], oh, False, True).then_inc(s_rk, 1)
                if s < NQ:
                    pe.wait_ge(s_otev, s)
                    for j in range(4):
                        tr = pe.transpose(bank[0][:, P * j:P * j + P], O[:, 4 * s + j, :], ident[:, :])
                    tr.then_inc(s_ot, 1)
                    pe.wait_ge(s_otev, s + 1)
                    pe.wait_ge(s_x2, s)
                    for j in range(4):
                        for b in (0, 1):
                            for r in (0, 1):
                                rows = slice(64 * b, 64 * b + 64)
                                op = mm(bank[1][rows, P * j:P * j + P],
                                        OT[rows, s % 2, P * j + 64 * r:P * j + 64 * r + 64], WO[rows, r, :],
                                        j == 0 and r == 0, r == 1)
                    op.then_inc(s_op, 1)
                if 1 <= s <= NQ:
                    q = s - 1
                    pe.wait_ge(s_xn2, q + 1)
                    pe.wait_ge(s_x2ev, q)
                    for j in range(4):
                        tr = pe.transpose(bank[2][:, P * j:P * j + P], XN[:, q % 2, j, :], ident[:, :])
                    tr.then_inc(s_x2t, 1)
                    pe.wait_ge(s_x2ev, q + 1)
                    pe.wait_ge(s_oh, q)
                    for j in range(4):
                        lgm = mm(bank[3][:, E * j:E * j + E], XN2T[:, q % 2, P * j:P * j + P], wr_sb[:, :], j == 0, True)
                    lgm.then_inc(s_lg, 1)

            def rows_in(s, u):
                pe.wait_ge(s_xg[u % R6], 16 * turn_of(u))
                pe.wait_ge(s_xtev, s)
                for k in (0, 1):
                    tr = pe.transpose(bank[6][:, :].bitcast(F16)[:, P * k:P * k + P], XG[:, u % R6, P * k:P * k + P],
                                      ident16[:, :])
                tr.then_inc(s_xt, 1)

            turns = {0: 1, 1: 2}

            def turn_of(u):
                return turns[u // R6]

            def gate_up(s, u):
                p = u % 2
                e = pe.value_load(tile_exp[0:1, bass.ds(s, 1)], min_val=0, max_val=E - 1)
                pe.wait_ge(s_xtev, s + 1)
                pe.wait_ge(s_h, s + 1)
                for n, (half, w) in enumerate(((0, 0), (0, 1), (1, 0))):
                    for gu in (0, 1):
                        g = mm(bank[2 * gu + p][:, :], XGT[:, p, half, :],
                               WG[:, bass.ds(e * 2048 + (1024 * w + 512 * gu), 512)], n == 0, n == 2)
                g.then_inc(s_gu, 1)

            def hidden_rows(s, u):
                p = u % 2
                pe.wait_ge(s_hl, s + 1)
                pe.wait_ge(s_htev, s + 1)
                for k in (0, 1):
                    for hc in range(HC):
                        at = H * k + P * hc
                        tr = pe.transpose(bank[4 + p][:, :].bitcast(F16)[:, at:at + P], HH[:, p, k, P * hc:P * hc + P],
                                          ident16[:, :])
                tr.then_inc(s_ht, 1)

            def down(s, u):
                p = u % 2
                e = pe.value_load(tile_exp[0:1, bass.ds(s, 1)], min_val=0, max_val=E - 1)
                pe.wait_ge(s_htev, s + 3)
                pe.wait_ge(s_yev, s)
                for hc in range(HC):
                    at = e * (HC * 256) + 256 * hc
                    mm(bank[7][:, 0:256], HT[:, p, 0, P * hc:P * hc + P], WD[:, bass.ds(at, 256)], hc == 0)
                    y = mm(bank[7][:, 0:P], HT[:, p, 1, P * hc:P * hc + P], WD[:, bass.ds(at, P)], False, hc == HC - 1)
                y.then_inc(s_y, 1)

            def ffn_step(s, u, gu, th, dn):
                if gu:
                    gate_up(s, u)
                if gu and gu != "last":
                    rows_in(s + 1, u + 1)
                if th:
                    hidden_rows(s - 1, u - 1)
                if dn:
                    down(s - 2, u - 2)

            pe.wait_ge(s_table, 2)
            pe.wait_ge(s_wl, E + 2)
            rows_in(0, 0)
            experts(pe, ffn_step, turns)

        @block.vector
        def _(dve):
            step = Chain(dve, s_dve)
            for s_ring, n in ((s_max, 2), (s_mt, 2), (s_exp, 2), (s_pl, 2), (s_pv, 2), (s_o, 2), (s_wl, 2),
                              (s_st, 8), (s_h, 2), (s_ht, 2), (s_hh, 2), (s_htev, 2), (s_y, 2)):
                dve.sem_inc(s_ring, n)
            dve.memset(ones_f[:, :], 1.0)
            dve.memset(QE[:, :, :, :, :].rearrange("p a r g t -> p (a r g t)").bitcast(F32), 0.0).then_inc(s_dconsts, 1)
            dve.memset(KS[:, :, :, :].rearrange("p a g t -> p (a g t)").bitcast(F32), 0.0).then_inc(s_dconsts, 1)
            dve.memset(runs[:, :], 0.0)
            dve.wait_ge(s_dconsts, 2)

            def norm_stats(src, t, ready):
                for j in range(4):
                    last = dve.bn_stats(stats[:, j, :], src[:, 4 * t + j, :])
                step(last)
                for j in range(4):
                    last = dve.bn_aggr(mv[:, j, :], stats[:, j, :])
                step(last)
                dve.tensor_scalar(ve[:, :], mv[:, :, 1], EPS, None, ALU.add).then_inc(ready, 1)

            def norm_apply(src, t, estimate, done):
                dve.wait_ge(estimate, t + 1)
                step(dve.tensor_tensor(nt[:, :], r0[:, :], r0[:, :], ALU.mult))
                step(dve.tensor_tensor(nt[:, :], nt[:, :], ve[:, :], ALU.mult))
                step(dve.tensor_scalar(nt[:, :], nt[:, :], -0.5, 1.5, ALU.mult, ALU.add))
                step(dve.tensor_tensor(nt[:, :], nt[:, :], r0[:, :], ALU.mult))
                for j in range(4):
                    last = dve.tensor_scalar(XN[:, t % 2, j, :], src[:, 4 * t + j, :], mv[:, j, 0:1], nt[:, j:j + 1],
                                             ALU.subtract, ALU.mult)
                last.then_inc(done, 1)

            def norm(t):
                dve.wait_ge(s_x[t % 2], 32 * (t // 2 + 1))
                norm_stats(X, t, s_var)
                norm_apply(X, t, s_rs, s_xn)

            dve.wait_ge(s_weights, 16 * N_W)
            for r in (0, 1):
                for dup in (0, 1):
                    last = dve.tensor_copy(woP[:, r, 64 * dup:64 * dup + 64].rearrange("o (g d) -> o g d", d=HD),
                                           w_nat[:, 3, :].rearrange("o (g r d) -> o r g d", r=2, d=HD)[:, r])
            last.then_inc(s_wperm, 1)
            dve.tensor_scalar(bqs_c[:, :], bq_c[:, :], SCALE, None, ALU.mult)
            dve.tensor_scalar(bvb[:, :], ones_f[:, :], bv_c[:, 0:1], None, ALU.mult).then_inc(s_wperm, 1)
            dve.wait_ge(s_wt, 3)
            dve.tensor_tensor(bias_row[:, :], bank[5][:, 0:P], bo_b[:, :], ALU.add).then_inc(s_bias, 1)

            def low(t):
                par = t % 2
                for n, bias in enumerate((bqs_c, bk_c)):
                    dve.wait_ge(s_hi, 3 * t + n + 1)
                    dve.scalar_tensor_tensor(out=QK[:, par, n, 1, :], in0=bank[2 + 2 * n + par][:, :],
                                             scalar=bias[:, 0:1], in1=QK[:, par, n, 0, :],
                                             op0=ALU.add, op1=ALU.subtract).then_inc(s_lo, 1)
                dve.wait_ge(s_hi, 3 * t + 3)
                dve.wait_ge(s_consts, N_CONST)
                for b in (0, 1):
                    rows = slice(64 * b, 64 * b + 64)
                    last = dve.tensor_tensor(VB[rows, 4 * t:4 * t + 4, :, 18 + 9 * b:26 + 9 * b],
                                             bank[6 + par][rows, :].rearrange("p (t h d) -> p t h d", t=4, d=HD),
                                             VB[rows, 4 * t:4 * t + 4, :, 9 * b:9 * b + 8], ALU.subtract)
                last.then_inc(s_lo, 1)

            norm(0)
            norm(1)
            for t in range(NQ):
                low(t)
                if t + 2 < NQ:
                    norm(t + 2)

            def lead(c, par, k, first):
                dve.wait_ge(s_mt, c + 1)
                for tt in (0, 1):
                    for b in (0, 1):
                        dve.wait_ge(s_sc, 4 * c + 2 * tt + b + 1)
                        dve.tensor_reduce(MX[:, par, :, 2 * tt + b], bank[b][:, :].rearrange("p (v k) -> p v k", k=64),
                                          AX.X, ALU.max).then_inc(s_max, 1)

            Ot = O[:, :, :].rearrange("p t n -> p (t n)")

            def normalise(t, tpar):
                dve.wait_ge(s_o, t + 2)
                dve.wait_ge(s_pv, t + 3)
                pv = bank[4 + tpar][:, 0:288].rearrange("p (v w) -> p v w", w=36)
                step(dve.tensor_copy(SM[:, :, :], pv[:, :, 18:36]))
                step(dve.tensor_tensor(SM[:, :, :], pv[:, :, 0:18], SM[:, :, :], ALU.add))
                sm = SM[:, :, :].rearrange("p v (b w) -> p v b w", b=2)
                step(dve.reciprocal(RS[:, :, :], sm[:, :, :, 8]))
                dve.tensor_tensor(Ot[:, bass.ds(t * P, P)].rearrange("p (b v d) -> p v b d", b=2, d=HD),
                                  sm[:, :, :, 0:8], RS[:, :, :].unsqueeze(3).to_broadcast([P, 8, 2, HD]),
                                  ALU.mult).then_inc(s_o, 1)

            def follow(c, par, k, first):
                for tt in (0, 1):
                    for gp in (0, 1):
                        m = 4 * c + 2 * tt + gp
                        half = slice(512 * gp, 512 * gp + 512)
                        dve.wait_ge(s_ph, m + 1)
                        dve.tensor_tensor(PL[:, tt, half], P32[:, gp, :], PH[:, tt, half], ALU.subtract).then_inc(s_pl, 1)
                    if not (first and tt == 0):
                        normalise(2 * c + tt - 1, 1 - tt)

            attention(LoopChain(dve, step, 12, 2), lead, follow, lambda: None)
            normalise(NT - 1, 1)

            dve.wait_ge(s_tanh, 1)
            step(dve.tensor_scalar(bias_row[:, :], bias_row[:, :], tg[:, 0:1], None, ALU.mult))
            step(dve.tensor_tensor(X[:, :, :], X[:, :, :], bias_row[:, :].unsqueeze(1).to_broadcast([P, NT, D]), ALU.add))
            dve.tensor_copy(jrow[:, :], jint[:, :])
            dve.tensor_scalar(tie[:, :], eint[:, :], -1.0, float(E), ALU.mult, ALU.add)
            step(dve.tensor_scalar(ebase[:, :], eint[:, :], float(N), None, ALU.mult))

            def first_of(oh, vals, top):
                b = lambda v: v[:, :].unsqueeze(2).to_broadcast([P, 4, E])
                step(dve.tensor_reduce(top[:, :], vals[:, :, :], AX.X, ALU.max))
                step(dve.tensor_tensor(oh[:, :, :], vals[:, :, :], b(top), ALU.is_equal))
                step(dve.tensor_tensor(oh[:, :, :], oh[:, :, :], tie[:, :].unsqueeze(1).to_broadcast([P, 4, E]), ALU.mult))
                step(dve.tensor_reduce(tm[:, :], oh[:, :, :], AX.X, ALU.max))
                step(dve.tensor_tensor(oh[:, :, :], oh[:, :, :], b(tm), ALU.is_equal))

            oh1s, oh2s = [oh1, oh1b], [oh2, oh2b]
            for s in range(NQ + 2):
                if s >= 2:
                    q = s - 2
                    par = q % 2
                    dve.wait_ge(s_rk, q + 1)
                    for j in range(4):
                        step(dve.tensor_tensor(rank[:, j, :], bank[4][:, E * j:E * j + E], runs[:, :], ALU.add))
                        step(dve.tensor_tensor(runs[:, :], runs[:, :], bank[4][:, 4 * E + E * j:4 * E + E * j + E], ALU.add))
                    step(dve.tensor_tensor(rank[:, :, :], rank[:, :, :], ebase[:, :].unsqueeze(1).to_broadcast([P, 4, E]),
                                           ALU.add))
                    for k, o in enumerate((oh1s[par], oh2s[par])):
                        step(dve.tensor_tensor(le[:, :, :], o[:, :, :], rank[:, :, :], ALU.mult))
                        step(dve.tensor_reduce(posf[:, k, :], le[:, :, :], AX.X, ALU.add))
                    if q >= 2:
                        dve.wait_ge(s_sent[par], 128)
                    dve.tensor_copy(pos[:, par, :, :], posf[:, :, :]).then_inc(s_pos, 1)
                if s < NQ:
                    t4 = slice(4 * s, 4 * s + 4)
                    dve.wait_ge(s_op, s + 1)
                    dve.scalar_tensor_tensor(out=X2[:, t4, :], in0=bank[1][:, :].rearrange("p (t n) -> p t n", n=D),
                                             scalar=tg[:, 0:1], in1=X[:, t4, :], op0=ALU.mult, op1=ALU.add)\
                       .then_inc(s_x2, 1)
                    dve.wait_ge(s_x2, s + 1)
                    norm_stats(X2, s, s_rv)
                    norm_apply(X2, s, s_rrs, s_xn2)
                    dve.wait_ge(s_xn2, s + 1)
                    par = s % 2
                    if s >= 2:
                        dve.wait_ge(s_sent[par], 128)
                    step(dve.tensor_copy(XHL[:, par, 0, :, 0:D], XN[:, par, :, :]))
                    step(dve.tensor_tensor(XHL[:, par, 0, :, D:2 * D], XN[:, par, :, :], XHL[:, par, 0, :, 0:D], ALU.subtract))
                    dve.tensor_copy(XHL[:, par, 1, :, 0:2 * D], XHL[:, par, 0, :, 0:2 * D])
                    for k in range(K):
                        last = dve.tensor_copy(XHL[:, par, k, :, 2 * D:XW].bitcast(I32), ids[:, t4, k:k + 1])
                    step(last)
                if 1 <= s <= NQ:
                    q = s - 1
                    o1, o2 = oh1s[q % 2], oh2s[q % 2]
                    dve.wait_ge(s_lg, q + 1)
                    step(dve.tensor_tensor(lg[:, :, :], bank[3][:, 0:4 * E].rearrange("p (t e) -> p t e", e=E),
                                           br_b[:, :].unsqueeze(1).to_broadcast([P, 4, E]), ALU.add))
                    first_of(o1, lg, m1)
                    step(dve.scalar_tensor_tensor(out=le[:, :, :], in0=o1[:, :, :], scalar=NEG, in1=lg[:, :, :],
                                                  op0=ALU.mult, op1=ALU.add))
                    first_of(o2, le, m2)
                    if q >= 1:
                        dve.wait_ge(s_rk, q)
                    dve.tensor_tensor(ohb[:, :, :], o1[:, :, :], o2[:, :, :], ALU.add).then_inc(s_oh, 1)
                    dve.tensor_tensor(m2[:, :], m2[:, :], m1[:, :], ALU.subtract).then_inc(s_gin, 1)
                    dve.wait_ge(s_gexp, q + 1)
                    step(dve.tensor_scalar(m1[:, :], m2[:, :], 1.0, None, ALU.add))
                    step(dve.reciprocal(m1[:, :], m1[:, :]))
                    t4 = slice(4 * q, 4 * q + 4)
                    step(dve.tensor_scalar(gw[:, t4, 0], m1[:, :], tg[:, 1:2], None, ALU.mult))
                    step(dve.tensor_tensor(gw[:, t4, 1], m2[:, :], gw[:, t4, 0], ALU.mult))

            one = lambda v: v[0:1, :]
            step(dve.tensor_scalar(cnt_i[:, :], one(runs), float(P - 1), None, ALU.add))
            step(dve.tensor_scalar(cnt_i[:, :], cnt_i[:, :], 7, None, ALU.logical_shift_right))
            step(dve.tensor_copy(cnt_f[:, :], cnt_i[:, :]))
            step(dve.tensor_tensor_scan(tiles_to[:, :], ones_f[0:1, 0:E], cnt_f[:, :], 0.0, ALU.mult, ALU.add))
            jb = jrow[:, :].unsqueeze(2).to_broadcast([1, FT, E])
            eb = lambda v: v[:, :].unsqueeze(1).to_broadcast([1, FT, E])
            step(dve.tensor_tensor(jge[:, :, :], jb, eb(tiles_to), ALU.is_ge))
            step(dve.tensor_reduce(jex[:, :], jge[:, :, :], AX.X, ALU.add))
            step(dve.tensor_tensor(jge[:, :, :], jge[:, :, :], eb(cnt_f), ALU.mult))
            step(dve.tensor_reduce(jbk[:, :], jge[:, :, :], AX.X, ALU.add))
            step(dve.tensor_tensor(jbk[:, :], jrow[:, :], jbk[:, :], ALU.subtract))
            step(dve.tensor_scalar(jbk[:, :], jbk[:, :], float(P), None, ALU.mult))
            dve.scalar_tensor_tensor(out=tile_row[:, 0:FT], in0=jex[:, :], scalar=float(N), in1=jbk[:, :],
                                     op0=ALU.mult, op1=ALU.add).then_inc(s_table, 1)
            dve.tensor_scalar(tile_exp[:, 0:FT], jex[:, :], float(E - 1), None, ALU.min).then_inc(s_table, 1)

            def rows_out(s, u):
                dve.wait_ge(s_xt, s + 1)
                if u >= 2:
                    dve.wait_ge(s_gu, s - 1)
                dve.tensor_copy(XGT[:, u % 2, :, :].rearrange("p k n -> p (k n)"), bank[6][:, :].bitcast(F16)[:, 0:256])\
                   .then_inc(s_xtev, 1)

            def ffn_step(s, u, gu, th, dn):
                p = u % 2
                if gu and gu != "last":
                    rows_out(s + 1, u + 1)
                if gu:
                    dve.wait_ge(s_silu, s + 1)
                    dve.wait_ge(s_hh, s + 1)
                    dve.tensor_tensor(HF[:, p, :], SG[:, p, :], bank[2 + p][:, :], ALU.mult).then_inc(s_h, 1)
                if dn:
                    dve.wait_ge(s_y, s + 1)
                    dve.tensor_copy(YT[:, :], bank[7][:, P:2 * P]).then_inc(s_yt, 1)
                    dve.wait_ge(s_yt, s - 1)
                    dve.tensor_tensor(YS[:, (u - 2) % R6, :], bank[7][:, 0:P], YT[:, :], ALU.add).then_inc(s_yev, 1)
                if gu:
                    dve.wait_ge(s_hh, s + 3)
                    dve.tensor_tensor(HH[:, p, 1, :], HF[:, p, :], HH[:, p, 0, :], ALU.subtract).then_inc(s_hl, 1)

            rows_out(0, 0)
            experts(dve, ffn_step)

            for q in range(NQ):
                dve.wait_ge(s_ya[q], 16)
                for k in range(K):
                    for j in range(4):
                        t = 4 * q + j
                        last = dve.scalar_tensor_tensor(out=X2[:, t, :], in0=YAk[q % 2][:, j, k, :],
                                                        scalar=gw[:, t, k:k + 1], in1=X2[:, t, :],
                                                        op0=ALU.mult, op1=ALU.add)
                    if k == 0:
                        step(last)
                last.then_inc(s_fin, 1)


_INS = ['x', 'ctx_1024', 'g_xattn', 'g_ffn', 'L0_xattn_wq', 'L0_xattn_bq', 'L0_xattn_wk', 'L0_xattn_bk', 'L0_xattn_wv',
        'L0_xattn_bv', 'L0_xattn_wo', 'L0_xattn_bo', 'L0_ffn_Wr', 'L0_ffn_br', 'L0_ffn_Wg', 'L0_ffn_Wu', 'L0_ffn_Wd']


def kernel(**inputs):
    import numpy as _np
    import concourse.bacc as _bacc
    from concourse import mybir as _mybir
    from concourse.bass_utils import run_bass_kernel_spmd as _run

    nc = _bacc.Bacc("TRN2", target_bir_lowering=False, num_devices=1)
    arrays, args = {}, []
    for name in _INS:
        a = _np.ascontiguousarray(inputs[name])
        arrays[f"in_{name}_dram"] = a
        args.append(nc.dram_tensor(f"in_{name}_dram", a.shape, _mybir.dt.from_np(a.dtype), kind="ExternalInput").ap())
    shape = inputs["x"].shape
    out = nc.dram_tensor("out_0_dram", shape, _mybir.dt.float32, kind="ExternalOutput").ap()
    flamingo_gated_block(nc, *args, out)
    r = _run(nc, [arrays], core_ids=[0])
    return r.results[0]["out_0_dram"]
```

```python
from contextlib import ExitStack, contextmanager

import concourse.bass as bass
from concourse import mybir

ALU = mybir.AluOpType
ACT = mybir.ActivationFunctionType
AX = mybir.AxisListType
F32 = mybir.dt.float32
F16 = mybir.dt.float16
BF16 = mybir.dt.bfloat16
I32 = mybir.dt.int32

P = 128
NEG = -1.0e30
EPS = 1.0e-5


class LoopChain:

    def __init__(self, eng, chain, steps, turns):
        self.eng, self.chain, self.steps, self.turns = eng, chain, steps, turns
        self.snap = eng.snap

    @contextmanager
    def Fori(self, start, end):
        with self.eng.Fori(start, end) as i:
            self.chain.turn(i - start, self.steps)
            yield i
        self.chain.end(self.turns)


class Chain:

    def __init__(self, eng, sem):
        self.eng, self.sem, self.base, self.n, self.steps = eng, sem, 0, 0, 0

    def __call__(self, instruction):
        instruction.then_inc(self.sem, 1)
        self.n += 1
        self.eng.wait_ge(self.sem, self.base + self.n)

    def turn(self, i, steps):
        self.start, self.steps = self.n, steps
        self.base = self.eng.snap(i * steps)

    def end(self, turns):
        assert self.n - self.start == self.steps, (self.n - self.start, self.steps)
        self.base, self.n = 0, self.start + self.steps * turns


def flamingo_gated_block(nc, x, ctx_in, g_xattn, g_ffn, wq, bq, wk, bk, wv, bv, wo, bo, Wr, br, Wg, Wu, Wd, out):
    B, T, D = x.shape
    E, _, H = Wg.shape
    HEADS = 16
    HD = D // HEADS
    SCALE = HD ** -0.5
    N = B * T
    NT = N // P
    NQ = NT // 4
    RS4 = 4
    HC = H // P
    K = 2
    FT = (N * K) // P + E - 1
    TRASH = E * N
    XROWS = TRASH + (FT - N * K // P) * P
    R6 = 6
    XW = 2 * D + 2
    assert (T, D, HD, HC, NQ, E, FT) == (64, P, 8, 4, 4, 8, 39)

    x_t = x.rearrange("(t b) q c -> (b q) t c", b=2)
    c_t = ctx_in.rearrange("(t b) q c -> (b q) t c", b=2)
    out_t = out.rearrange("(t b) q c -> (b q) t c", b=2)

    with ExitStack() as ctx:
        def sb(name, shape, dt):
            return ctx.enter_context(nc.sbuf_tensor(name, shape, dt))

        def sem(name):
            return ctx.enter_context(nc.semaphore(name))

        def dram(name, shape, dt):
            return nc.dram_tensor(name, shape, dt, kind="Internal").ap()

        q_parts = dram("q_parts", [3, HD, HEADS, N], F16)
        k_parts = dram("k_parts", [3, HD, HEADS, N], F16)
        routed = dram("routed", [XROWS, XW], F16)
        expert_out = dram("expert_out", [N * K, D], F32)

        X = sb("X", [P, NT, D], F32)
        C = sb("C", [P, NT, D], F32)
        XN = sb("XN", [P, 2, 4, D], F32)
        xT = sb("xT", [P, 2, 512], F32)
        cT = sb("cT", [P, 2, 512], F32)
        QK = sb("QK", [P, 2, 2, 2, 512], F16)
        w_nat = sb("w_nat", [P, 4, D], F32)
        wqT = sb("wqT", [P, D], F32)
        wkT = sb("wkT", [P, D], F32)
        wvT = sb("wvT", [P, D], F32)
        woT = sb("woT", [P, D], F32)
        woP = sb("woP", [P, 2, P], F32)
        WO = sb("WO", [P, 2, D], F32)
        bq_c = sb("bq_c", [P, 1], F32)
        bqs_c = sb("bqs_c", [P, 1], F32)
        bk_c = sb("bk_c", [P, 1], F32)
        bv_c = sb("bv_c", [P, 1], F32)
        bvb = sb("bvb", [P, P], F32)
        bo_b = sb("bo_b", [P, D], F32)
        bias_row = sb("bias_row", [P, D], F32)
        br_b = sb("br_b", [P, E], F32)
        wr_sb = sb("wr_sb", [P, E], F32)
        gx = sb("gx", [P, 2], F32)
        tg = sb("tg", [P, 2], F32)
        ident = sb("ident", [P, P], F32)
        ident16 = sb("ident16", [P, P], F16)
        identb = sb("identb", [P, P], BF16)
        ones_f = sb("ones_f", [P, P], F32)
        mask_q = sb("mask_q", [P, 64], BF16)
        shift_w = sb("shift_w", [80, 8, P], BF16)
        shift_m = sb("shift_m", [80, 2, P], BF16)
        before = sb("before", [P, P], BF16)
        ones_b = sb("ones_b", [P, P], BF16)
        QE = sb("QE", [P, RS4, 4, 4, P], F16)
        KS = sb("KS", [P, RS4, 4, P], F16)
        VB = sb("VB", [P, NT, HEADS, 36], F16)
        VR = sb("VR", [P, 2, HEADS * 36], F16)
        VRw = VR[:, :, :].rearrange("p a n -> p (a n)").bitcast(F32).rearrange("p (a n) -> p a n", a=2)
        VBw = VB[:, :, :, :].rearrange("p t h w -> p (t h w)").bitcast(F32)
        MX = sb("MX", [P, 2, 8, 2], F32)
        P32 = sb("P32", [P, 2, 512], F32)
        PH = sb("PH", [P, 2, 1024], F16)
        PL = sb("PL", [P, 2, 1024], F16)
        SM = sb("SM", [P, 8, 18], F32)
        RS = sb("RS", [P, 8, 2], F32)
        O = sb("O", [P, NT, D], F32)
        stats = sb("stats", [P, 4, 6], F32)
        mv = sb("mv", [P, 4, 2], F32)
        ve = sb("ve", [P, 4], F32)
        lnv = sb("lnv", [P, 4], F32)
        r0 = sb("r0", [P, 4], F32)
        nt = sb("nt", [P, 4], F32)
        X2 = C
        OT = xT
        XN2T = cT
        ids = sb("ids", [P, NT, K], I32)
        XHL = sb("XHL", [P, 2, K, 4, XW], F16)
        lg = sb("lg", [P, 4, E], F32)
        le = sb("le", [P, 4, E], F32)
        tie = sb("tie", [P, E], F32)
        ebase = sb("ebase", [P, E], F32)
        m1 = sb("m1", [P, 4], F32)
        m2 = sb("m2", [P, 4], F32)
        tm = sb("tm", [P, 4], F32)
        oh1 = sb("oh1", [P, 4, E], F32)
        oh2 = sb("oh2", [P, 4, E], F32)
        oh1b = sb("oh1b", [P, 4, E], F32)
        oh2b = sb("oh2b", [P, 4, E], F32)
        ohb = sb("ohb", [P, 4, E], BF16)
        rank = sb("rank", [P, 4, E], F32)
        posf = sb("posf", [P, K, 4], F32)
        pos = sb("pos", [P, 2, K, 4], I32)
        runs = sb("runs", [P, E], F32)
        gw = sb("gw", [P, NT, K], F32)
        cnt_i = sb("cnt_i", [1, E], I32)
        cnt_f = sb("cnt_f", [1, E], F32)
        tiles_to = sb("tiles_to", [1, E], F32)
        eint = sb("eint", [P, E], I32)
        jint = sb("jint", [1, FT], I32)
        jrow = sb("jrow", [1, FT], F32)
        jge = sb("jge", [1, FT, E], F32)
        jex = sb("jex", [1, FT], F32)
        jbk = sb("jbk", [1, FT], F32)
        tile_row = sb("tile_row", [1, FT + 1], I32)
        tile_base = sb("tile_base", [1, FT + 9], I32)
        fill = sb("fill", [P, 5, XW], F16)
        WS = sb("WS", [P, 2, 3, 512], F32)
        EW = 4 * H + 2 * D * HC
        WE = sb("WE", [P, E * EW], F16)

        XG = sb("XG", [P, R6, XW], F16)
        XGT = sb("XGT", [P, 2, 2, P], F16)
        YT = sb("YT", [P, 2, D], F32)
        QEf = QE[:, :, :, :, :].rearrange("p a r g t -> p (a r g t)").bitcast(F32)
        SG = QEf[:, 0:2 * H].rearrange("p (a n) -> p a n", a=2)
        HF = QEf[:, 2 * H:4 * H].rearrange("p (a n) -> p a n", a=2)
        HH = sb("HH", [P, 2, 2, H], F16)
        HT = sb("HT", [P, 2, 2, H], F16)
        YS = sb("YS", [P, R6, D], F32)
        YA = O
        bank = [ctx.enter_context(nc.psum_tensor(f"bank{i}", [P, 512], F32)) for i in range(8)]


        def down_half(e, k):
            w = WE[:, bass.ds(e * EW + 4 * H, 2 * D * HC)]
            return w.rearrange("p (h k n) -> p k h n", h=HC, k=2)[:, k]

        parts_q = q_parts.rearrange("c d (g r) t -> r (c d) g t", r=4)
        parts_k = k_parts.rearrange("c d (g r) t -> r (c d) g t", r=4)

        s_weights = sem("s_weights")
        s_x = [sem("s_x0"), sem("s_x1")]
        s_pool = sem("s_pool")
        s_turns = sem("s_turns")
        s_yt = sem("s_yt")
        s_consts = sem("s_consts")
        s_dconsts = sem("s_dconsts")
        s_fill = sem("s_fill")
        s_wt = sem("s_wt")
        s_wev = sem("s_wev")
        s_wperm = sem("s_wperm")
        s_tanh = sem("s_tanh")
        s_bias = sem("s_bias")
        s_dve = sem("s_dve")
        s_act = sem("s_act")
        s_var = sem("s_var")
        s_rs = sem("s_rs")
        s_xn = sem("s_xn")
        s_tr = sem("s_tr")
        s_trev = sem("s_trev")
        s_qkv = sem("s_qkv")
        s_hi = sem("s_hi")
        s_lo = sem("s_lo")
        s_parts = [sem("s_parts0"), sem("s_parts1")]
        s_stack = [sem(f"s_stack{i}") for i in range(RS4)]
        s_sc = [sem("s_sc0"), sem("s_sc1")]
        s_max = sem("s_max")
        s_mt = sem("s_mt")
        s_shift = sem("s_shift")
        s_st = [sem("s_st0"), sem("s_st1")]
        s_exp = [sem("s_exp0"), sem("s_exp1")]
        s_vr = sem("s_vr")
        s_ph = [sem("s_ph0"), sem("s_ph1")]
        s_pl = [sem("s_pl0"), sem("s_pl1")]
        s_pv = sem("s_pv")
        s_o = sem("s_o")
        s_ws = [sem("s_ws0"), sem("s_ws1")]
        s_wh = [sem("s_wh0"), sem("s_wh1")]
        s_wl = [sem("s_wl0"), sem("s_wl1")]
        s_ot = sem("s_ot")
        s_otev = sem("s_otev")
        s_op = sem("s_op")
        s_x2 = sem("s_x2")
        s_rv = sem("s_rv")
        s_rrs = sem("s_rrs")
        s_xn2 = sem("s_xn2")
        s_x2t = sem("s_x2t")
        s_x2ev = sem("s_x2ev")
        s_lg = sem("s_lg")
        s_gexp = sem("s_gexp")
        s_gin = sem("s_gin")
        s_oh = sem("s_oh")
        s_rk = sem("s_rk")
        s_pos = sem("s_pos")
        s_sent = [sem("s_sent0"), sem("s_sent1")]
        s_table = sem("s_table")
        s_xg = [sem(f"s_xg{i}") for i in range(R6)]
        s_xt = sem("s_xt")
        s_xt0 = sem("s_xt0")
        s_xtev = sem("s_xtev")
        s_gu = sem("s_gu")
        s_silu = sem("s_silu")
        s_h = sem("s_h")
        s_hh = sem("s_hh")
        s_hl = sem("s_hl")
        s_ht = sem("s_ht")
        s_htev = sem("s_htev")
        s_y = sem("s_y")
        s_yev = sem("s_yev")
        s_ysent = [sem(f"s_ysent{i}") for i in range(R6)]
        s_ya = [sem(f"s_ya{i}") for i in range(4)]
        s_fin = sem("s_fin")
        s_out = sem("s_out")

        N_CONST = 15
        N_W = 4 + 2 * HD + 6
        block = ctx.enter_context(nc.Block())

        def experts(eng, ffn_step, bases=None):
            load = bases or (lambda first, n, turn: None)
            load(0, 2, 0)
            ffn_step(0, 0, 0, True, False, False)
            ffn_step(1, 1, 0, True, True, False)
            with eng.Fori(0, R6) as turn:
                i = eng.snap(turn * R6)
                load(i, R6 + 2, turn)
                for u in range(2, 2 + R6):
                    ffn_step(i + u, u, i, True, True, True)
            load(FT - 3, 3, R6)
            ffn_step(FT - 1, 2, R6 * R6, "last", True, True)
            ffn_step(FT, 3, R6 * R6, False, True, True)
            ffn_step(FT + 1, 4, R6 * R6, False, False, True)

        def attention(eng, lead, follow):
            def steps(t0, i):
                for u in range(4):
                    if not isinstance(t0, int) or t0 + u + 2 < NT:
                        lead(t0 + u + 2, (u + 2) % 4, i + (u + 2) // 4)
                    follow(t0 + u, u, i)

            lead(0, 0, 0)
            lead(1, 1, 0)
            steps(0, 0)
            with eng.Fori(1, NQ - 1) as i:
                steps(eng.snap(4 * i), i)
            steps(NT - 4, NQ - 1)

        YAf = [O[:, 8 * i:8 * i + 8, :] for i in (0, 1)]
        YAq = [v.rearrange("p (t k) n -> p t (k n)", k=K) for v in YAf]
        YAk = [v.rearrange("p (t k) n -> p t k n", k=K) for v in YAf]

        @block.sync
        def _(sp):
            for t in range(NQ):
                if t >= 2:
                    sp.wait_ge(s_x[t % 2], 32)
                sp.dma_start(X[:, 4 * t:4 * t + 4, :], x_t[:, 4 * t:4 * t + 4, :]).then_inc(s_x[t % 2], 16)
                sp.dma_start(C[:, 4 * t:4 * t + 4, :], c_t[:, 4 * t:4 * t + 4, :]).then_inc(s_x[t % 2], 16)
                if t == 0:
                    for n, w in enumerate((wq, wk, wv, wo)):
                        sp.dma_start(w_nat[:, n, :], w).then_inc(s_weights, 16)
                    for b_dram, b_sb in ((bq, bq_c), (bk, bk_c)):
                        by_d = b_dram.rearrange("(h d o) -> d h o", d=HD, o=1)
                        for d in range(HD):
                            sp.dma_start(b_sb[HEADS * d:HEADS * (d + 1), :], by_d[d],
                                         allow_slow_non_contiguous=True).then_inc(s_weights, 16)
                    sp.dma_start(bv_c[:, :], bv.rearrange("(p o) -> p o", o=1)).then_inc(s_weights, 16)
                    sp.dma_start(bo_b[:, :], bo.partition_broadcast(P)).then_inc(s_weights, 16)
                    sp.dma_start(br_b[:, :], br.partition_broadcast(P)).then_inc(s_weights, 16)
                    sp.dma_start(wr_sb[:, :], Wr).then_inc(s_weights, 16)
                    sp.dma_start(gx[:, 0:1], g_xattn.partition_broadcast(P)).then_inc(s_weights, 16)
                    sp.dma_start(gx[:, 1:2], g_ffn.partition_broadcast(P)).then_inc(s_weights, 16)

            def write_parts(t, par):
                sp.wait_ge(s_lo, 3 * t + 2)
                for n, (parts, order) in enumerate(((q_parts, (0, 0, 1)), (k_parts, (0, 1, 0)))):
                    for c, half in enumerate(order):
                        sp.dma_start(parts[c].rearrange("d h t -> (d h) t")[:, bass.ds(t * 512, 512)],
                                     QK[:, par, n, half, :]).then_inc(s_parts[par], 16)

            def load_stack(t, u):
                for r in range(4):
                    sp.dma_start(QE[32 * r:32 * r + 24, u, r, :, :],
                                 parts_q[r][:, :, bass.ds(t * P, P)]).then_inc(s_stack[u], 16)
                    sp.dma_start(KS[32 * r:32 * r + 24, u, :, :],
                                 parts_k[r][:, :, bass.ds(t * P, P)]).then_inc(s_stack[u], 16)

            def load_expert(e, par):
                sp.dma_start(WS[:, par, 0, :], Wg[bass.ds(e, 1)].rearrange("o d h -> (o d) h")).then_inc(s_ws[par], 16)
                sp.dma_start(WS[:, par, 1, :], Wu[bass.ds(e, 1)].rearrange("o d h -> (o d) h")).then_inc(s_ws[par], 16)
                sp.dma_start(WS[:, par, 2, :].rearrange("p (c n) -> p c n", c=HC),
                             Wd[bass.ds(e, 1)].rearrange("o (c p) n -> p (o c) n", p=P)).then_inc(s_ws[par], 16)

            sp.wait_ge(s_dconsts, 2)
            write_parts(0, 0)
            sp.wait_ge(s_parts[0], 96)
            for u in range(RS4):
                load_stack(u, u)
            write_parts(1, 1)
            write_parts(2, 0)
            write_parts(3, 1)
            load_expert(0, 0)
            load_expert(1, 1)
            for p_ in (0, 1):
                sp.wait_ge(s_parts[p_], 2 * 96)
            sp.wait_ge(s_consts, N_CONST)
            r_fill = routed.rearrange("(n p m) w -> n p (m w)", p=P, m=5)
            with sp.Fori(0, NQ - 1) as i:
                for u in range(RS4):
                    sp.wait_ge(s_st[1], 4 * i + u + 1)
                    load_stack(4 * i + u + 4, u)
                    if u >= 2:
                        sp.wait_ge(s_wl[u - 2], i + 1)
                        load_expert(2 * i + u, u - 2)
            for n in range(r_fill.shape[0]):
                sp.dma_start(r_fill[n], fill[:, :, :].rearrange("p m w -> p (m w)")).then_inc(s_fill, 16)

            sp.wait_ge(s_fill, 16 * r_fill.shape[0])
            sp.wait_ge(s_sent[0], 2 * 8 * 16)
            sp.wait_ge(s_sent[1], 2 * 8 * 16)
            sp.wait_ge(s_table, 2)

            def load_rows(j, u):
                row = sp.value_load(tile_row[0:1, bass.ds(j, 1)], min_val=0, max_val=XROWS - P)
                sp.dma_start(XG[:, u, :], routed[bass.ds(row, P), :]).then_inc(s_xg[u], 16)

            for j in range(R6):
                load_rows(j, j)
            with sp.Fori(1, 6) as i:
                for u in range(R6):
                    sp.wait_ge(s_ysent[u], i * 16)
                    load_rows(R6 * i + u, u)
            for u in range(FT - 6 * R6):
                sp.wait_ge(s_ysent[u], 6 * 16)
                load_rows(6 * R6 + u, u)
            for u in range(R6):
                sp.wait_ge(s_ysent[u], 16 * (7 if u < FT - 6 * R6 else 6))
            r_out = expert_out[0:N * K, :].rearrange("(t p k) n -> p t (k n)", p=P, k=K)
            for q in range(NQ):
                if q >= 2:
                    sp.wait_ge(s_fin, q - 1)
                sp.dma_start(YAq[q % 2], r_out[:, 4 * q:4 * q + 4, :]).then_inc(s_ya[q], 16)
            for q in range(NQ):
                sp.wait_ge(s_fin, q + 1)
                sp.dma_start(out_t[:, 4 * q:4 * q + 4, :], X2[:, 4 * q:4 * q + 4, :]).then_inc(s_out, 16)
            sp.wait_ge(s_out, 16 * NQ)


        @block.gpsimd
        def _(pool):
            pool.memset(ident[:, :], 0.0)
            pool.memset(ident16[:, :], 0.0)
            pool.memset(identb[:, :], 0.0)
            pool.memset(mask_q[:, :], 0.0)
            pool.memset(shift_w[:, :, :], 0.0)
            pool.memset(shift_m[:, :, :], 0.0)
            pool.memset(before[:, :], 1.0)
            pool.memset(ones_b[:, :], 1.0)
            pool.memset(VB[:, :, :, :].rearrange("p t h w -> p (t h w)").bitcast(F32), 0.0)
            pool.memset(fill[:, :, :].rearrange("p m w -> p (m w)").bitcast(F32), 0.0).then_inc(s_pool, 1)
            pool.wait_ge(s_pool, 1)
            const = Chain(pool, s_consts)
            for t in (ident, ident16, identb):
                const(pool.affine_select(out=t[:, :], in_=t[:, :], compare_op=ALU.not_equal, fill=1.0,
                                   base=0, pattern=[[-1, P]], channel_multiplier=1))
            for r in (0, 1):
                m = mask_q[64 * r:64 * r + 64, :]
                const(pool.affine_select(out=m, in_=m, compare_op=ALU.is_ge, fill=NEG,
                                   base=0, pattern=[[-1, 64]], channel_multiplier=1))
            m = shift_w[0:64, :, :].rearrange("p v (b k) -> p (v b) k", b=2)
            const(pool.affine_select(out=m, in_=m, compare_op=ALU.is_ge, fill=NEG,
                               base=0, pattern=[[0, 16], [-1, 64]], channel_multiplier=1))
            m = shift_w[64:80, :, :].rearrange("p v (b k) -> p v b k", b=2)
            const(pool.affine_select(out=m, in_=m, compare_op=ALU.not_equal, fill=1.0,
                               base=0, pattern=[[-2, 8], [-1, 2], [0, 64]], channel_multiplier=1))
            m = shift_m[0:64, :, :].rearrange("p a (b k) -> p (a b) k", b=2)
            const(pool.affine_select(out=m, in_=m, compare_op=ALU.not_equal, fill=1.0,
                               base=0, pattern=[[0, 4], [-1, 64]], channel_multiplier=1))
            const(pool.affine_select(out=before[:, :], in_=before[:, :], compare_op=ALU.is_gt, fill=0.0,
                               base=0, pattern=[[1, P]], channel_multiplier=-1))
            const(pool.memset(VB[0:64, :, :, 8:9], 1.0))
            const(pool.memset(VB[64:P, :, :, 17:18], 1.0))
            const(pool.iota(ids[:, :, :], pattern=[[2 * P, NT], [1, K]], channel_multiplier=2))
            const(pool.iota(eint[:, :], pattern=[[1, E]], channel_multiplier=0))
            const(pool.iota(jint[:, :], pattern=[[1, FT]], channel_multiplier=0))
            const(pool.memset(fill[:, :, 2 * D:XW].bitcast(I32), N * K))

            def low_halves(e, par):
                g_hi, u_lo = WE[:, bass.ds(e * EW, 2 * H)], WE[:, bass.ds(e * EW + 2 * H, 2 * H)]
                pool.tensor_tensor(u_lo, WS[:, par, 0:2, :].rearrange("p k n -> p (k n)"), g_hi, ALU.subtract)
                pool.tensor_tensor(down_half(e, 1),
                                   WS[:, par, 2, :].rearrange("p (h n) -> p h n", h=HC),
                                   down_half(e, 0),
                                   ALU.subtract).then_inc(s_wl[par], 1)

            def lead(t, u, i):
                if not (isinstance(t, int) and t < 2):
                    pool.wait_ge(s_pv, t - 1)
                pool.tensor_copy(VRw[:, u % 2, :], VBw[:, bass.ds(t * 288, 288)]).then_inc(s_vr, 1)

            def follow(t, u, i):
                if u % 2:
                    pool.wait_ge(s_wh[u // 2], i + 1)
                    low_halves(2 * i + u // 2, u // 2)

            pool.wait_ge(s_lo, 3 * NQ)
            attention(pool, lead, follow)

            pool.wait_ge(s_fill, 16 * 27)
            for q in range(NQ):
                par = q % 2
                pool.wait_ge(s_pos, q + 1)
                for k in range(K):
                    for j in range(4):
                        pool.indirect_dma_start(
                            out=routed[:, :], out_offset=bass.IndirectOffsetOnAxis(ap=pos[:, par, k, j:j + 1], axis=0),
                            in_=XHL[:, par, k, j, :], in_offset=None).then_inc(s_sent[par], 16)

            last_row = pool.to_reg(N * K - 1)

            def scatter(j, u):
                pool.wait_ge(s_table, 2)
                pool.wait_ge(s_yev, j + 1)
                pool.sem_inc(s_turns, 1)
                pool.indirect_dma_start(
                    out=expert_out[:, :],
                    out_offset=bass.IndirectOffsetOnAxis(ap=XG[:, u, 2 * D:XW].bitcast(I32), axis=0),
                    in_=YS[:, u, :], in_offset=None,
                    bounds_check=last_row, oob_is_err=False).then_inc(s_ysent[u], 16)

            with pool.Fori(0, 6) as i:
                for u in range(R6):
                    scatter(R6 * i + u, u)
            for u in range(FT - 6 * R6):
                scatter(6 * R6 + u, u)

        @block.scalar
        def _(act):
            step = Chain(act, s_act)

            act.wait_ge(s_wt, 1)
            act.activation(wqT[:, :].rearrange("c (d h) -> c h d", d=HD),
                           bank[0][:, 0:P].rearrange("c (h d) -> c h d", d=HD), ACT.Copy, scale=SCALE).then_inc(s_wev, 1)
            act.activation(wkT[:, :].rearrange("c (d h) -> c h d", d=HD),
                           bank[1][:, 0:P].rearrange("c (h d) -> c h d", d=HD), ACT.Copy).then_inc(s_wev, 1)
            act.activation(wvT[:, :], bank[2][:, 0:P], ACT.Copy).then_inc(s_wev, 1)
            act.activation(woT[:, :], bank[3][:, 0:P], ACT.Copy).then_inc(s_wev, 1)
            act.wait_ge(s_wt, 2)
            for r in (0, 1):
                act.activation(WO[:, r, :], bank[4][:, r * P:r * P + P], ACT.Copy).then_inc(s_wev, 1)
            act.wait_ge(s_weights, 16 * N_W)
            act.activation(tg[:, :], gx[:, :], ACT.Tanh).then_inc(s_tanh, 1)

            def rsqrt(v_ready, n, done):
                act.wait_ge(v_ready, n)
                step(act.activation(lnv[:, :], ve[:, :], ACT.Ln))
                act.activation(r0[:, :], lnv[:, :], ACT.Exp, scale=-0.5).then_inc(done, 1)

            rsqrt(s_var, 1, s_rs)
            rsqrt(s_var, 2, s_rs)
            for t in range(NQ):
                par = t % 2
                act.wait_ge(s_tr, 2 * t + 1)
                act.activation(xT[:, par, :], bank[0][:, :], ACT.Copy).then_inc(s_trev, 1)
                act.wait_ge(s_tr, 2 * t + 2)
                act.activation(cT[:, par, :], bank[1][:, :], ACT.Copy).then_inc(s_trev, 1)
                if t >= 2:
                    act.wait_ge(s_parts[par], 96)
                act.wait_ge(s_qkv, 3 * t + 1)
                act.activation(QK[:, par, 0, 0, :], bank[2 + par][:, :], ACT.Identity, bias=bqs_c[:, 0:1]).then_inc(s_hi, 1)
                act.wait_ge(s_qkv, 3 * t + 2)
                act.activation(QK[:, par, 1, 0, :], bank[4 + par][:, :], ACT.Identity, bias=bk_c[:, 0:1]).then_inc(s_hi, 1)
                act.wait_ge(s_qkv, 3 * t + 3)
                for b in (0, 1):
                    rows = slice(64 * b, 64 * b + 64)
                    v = act.activation(VB[rows, 4 * t:4 * t + 4, :, 9 * b:9 * b + 8],
                                       bank[6 + par][rows, :].rearrange("p (t h d) -> p t h d", t=4, d=HD), ACT.Copy)
                v.then_inc(s_hi, 1)
                if t + 2 < NQ:
                    rsqrt(s_var, t + 3, s_rs)

            def shift(u):
                act.activation(shift_m[64:80, u % 2, :], bank[6][0:16, 0:P], ACT.Copy, scale=-1.0).then_inc(s_shift, 1)

            def lead(t, u, i):
                if isinstance(t, int) and t == 1:
                    act.wait_ge(s_mt, 1)
                    shift(0)

            def follow(t, u, i):
                later = not (isinstance(t, int) and t == 0)
                for gp in (0, 1):
                    act.wait_ge(s_st[gp], t + 1)
                    if later:
                        act.wait_ge(s_pl[gp], t)
                    act.activation(P32[:, gp, :], bank[2 + gp][:, :], ACT.Exp).then_inc(s_exp[gp], 1)
                    act.wait_ge(s_exp[gp], t + 1)
                    act.activation(PH[:, u % 2, 512 * gp:512 * gp + 512], P32[:, gp, :], ACT.Copy).then_inc(s_ph[gp], 1)
                if not (isinstance(t, int) and t == NT - 1):
                    shift(u + 1)
                if u % 2:
                    par = u // 2
                    act.wait_ge(s_ws[par], 48 * (i + 1))
                    act.activation(WE[:, bass.ds((2 * i + par) * EW, 2 * H)],
                                   WS[:, par, 0:2, :].rearrange("p k n -> p (k n)"), ACT.Copy)
                    act.activation(down_half(2 * i + par, 0),
                                   WS[:, par, 2, :].rearrange("p (h n) -> p h n", h=HC), ACT.Copy).then_inc(s_wh[par], 1)

            attention(act, lead, follow)

            for s in range(NQ + 1):
                if s < NQ:
                    act.wait_ge(s_ot, s + 1)
                    if s >= 2:
                        act.wait_ge(s_op, s - 1)
                    act.activation(OT[:, s % 2, :], bank[0][:, :], ACT.Copy).then_inc(s_otev, 1)
                    rsqrt(s_rv, s + 1, s_rrs)
                if s >= 1:
                    q = s - 1
                    act.wait_ge(s_x2t, q + 1)
                    act.activation(XN2T[:, q % 2, :], bank[2][:, :], ACT.Copy).then_inc(s_x2ev, 1)
                    act.wait_ge(s_gin, q + 1)
                    act.activation(m2[:, :], m2[:, :], ACT.Exp).then_inc(s_gexp, 1)

            def silu(s, p):
                act.wait_ge(s_gu, s + 1)
                act.activation(SG[:, p, :], bank[p][:, :], ACT.Silu).then_inc(s_silu, 1)

            def high(s, p):
                act.wait_ge(s_h, s + 1)
                act.activation(HH[:, p, 0, :], HF[:, p, :], ACT.Copy).then_inc(s_hh, 1)

            def hidden_out(s, p):
                act.wait_ge(s_ht, s + 2)
                act.activation(HT[:, p, :, :].rearrange("p k n -> p (k n)"), bank[4 + p][:, :].bitcast(F16), ACT.Copy)\
                   .then_inc(s_htev, 1)

            def ffn_step(s, u, i, gu, th, dn):
                if gu:
                    silu(s, u % 2)
                    high(s, u % 2)
                if th:
                    hidden_out(s - 1, (u + 1) % 2)

            experts(act, ffn_step)

        @block.tensor
        def _(pe):
            def mm(o, a, b, start, stop=False):
                return pe.matmul(o, a, b, start=start, stop=stop, skip_group_check=True)

            pe.wait_ge(s_consts, N_CONST)
            pe.wait_ge(s_weights, 16 * N_W)
            for n in range(4):
                tr = pe.transpose(bank[n][:, 0:P], w_nat[:, n, :], ident[:, :])
            tr.then_inc(s_wt, 1)
            pe.wait_ge(s_wperm, 1)
            for r in (0, 1):
                tr = pe.transpose(bank[4][:, r * P:r * P + P], woP[:, r, :], ident[:, :])
            tr.then_inc(s_wt, 1)
            pe.wait_ge(s_wev, 4)
            pe.wait_ge(s_wperm, 2)
            mm(bank[5][:, 0:P], bvb[:, :], woT[:, :], True, True).then_inc(s_wt, 1)
            pe.wait_ge(s_wev, 6)
            pe.wait_ge(s_bias, 1)

            for t in range(NQ):
                par = t % 2
                pe.wait_ge(s_xn, t + 1)
                pe.wait_ge(s_trev, 2 * t)
                for j in range(4):
                    tr = pe.transpose(bank[0][:, P * j:P * j + P], XN[:, par, j, :], ident[:, :])
                tr.then_inc(s_tr, 1)
                pe.wait_ge(s_x[par], 32 * (t // 2 + 1))
                for j in range(4):
                    tr = pe.transpose(bank[1][:, P * j:P * j + P], C[:, 4 * t + j, :], ident[:, :])
                tr.then_inc(s_tr, 1)
                if t >= 2:
                    pe.wait_ge(s_lo, 3 * (t - 1))
                pe.wait_ge(s_trev, 2 * t + 1)
                mm(bank[2 + par][:, :], wqT[:, :], xT[:, par, :], True, True).then_inc(s_qkv, 1)
                pe.wait_ge(s_trev, 2 * t + 2)
                mm(bank[4 + par][:, :], wkT[:, :], cT[:, par, :], True, True).then_inc(s_qkv, 1)
                for j in range(4):
                    v = mm(bank[6 + par][:, P * j:P * j + P], cT[:, par, P * j:P * j + P], wvT[:, :], j == 0, True)
                v.then_inc(s_qkv, 1)
            pe.wait_ge(s_lo, 3 * NQ)

            def max_rows(u):
                pe.transpose(bank[6][0:16, 0:P], MX[:, u % 2, :, :].rearrange("p v b -> p (v b)"), ident[:, :])\
                  .then_inc(s_mt, 1)

            def lead(t, u, i):
                first = isinstance(t, int) and t == 0
                pe.wait_ge(s_stack[u], 128 * (i + 1))
                if not first:
                    pe.wait_ge(s_max, t)
                for b in (0, 1):
                    toks = slice(64 * b, 64 * b + 64)
                    mm(bank[b][:, :], identb[:, :], mask_q[:, :].unsqueeze(1).to_broadcast([P, 8, 64]), True)
                    for rp in (0, 1):
                        for g in range(4):
                            at = 64 * (4 * rp + g)
                            for r in (0, 1):
                                sc = mm(bank[b][64 * r:64 * r + 64, at:at + 64], QE[:, u, 2 * rp + r, g, toks],
                                        KS[:, u, g, toks], False, True)
                    sc.then_inc(s_sc[b], 1)
                if isinstance(t, int) and t == 1:
                    max_rows(0)

            def products(t, u):
                tpar = u % 2
                pe.wait_ge(s_vr, t + 1)
                pe.wait_ge(s_pl[1], t + 1)
                for g in range(4):
                    for r in range(4):
                        r1, at = 64 * (r % 2), 36 * (2 * g + r // 2)
                        col, at_v = 256 * g + 64 * r, 36 * (4 * g + r)
                        mm(bank[4 + tpar][r1:r1 + 64, at:at + 36], PH[:, tpar, col:col + 64], VR[:, tpar, at_v:at_v + 36],
                           g == 0 and r < 2)
                        pv = mm(bank[4 + tpar][r1:r1 + 64, at:at + 18], PL[:, tpar, col:col + 64], VR[:, tpar, at_v:at_v + 18], False, True)
                pv.then_inc(s_pv, 1)

            def follow(t, u, i):
                pe.wait_ge(s_shift, t + 1)
                end = t if isinstance(t, int) else 0
                if end == NT - 2:
                    pe.wait_ge(s_max, NT)
                if end < NT - 1:
                    max_rows(u + 1)
                for gp in (0, 1):
                    for g2 in (0, 1):
                        for rp in (0, 1):
                            at = 256 * g2 + 128 * rp
                            mm(bank[2 + gp][:, at:at + P], shift_w[:, 4 * rp + 2 * gp + g2, :],
                               shift_m[:, u % 2, :], g2 == 0 and rp == 0)
                    for g2 in (0, 1):
                        for b in (0, 1):
                            toks = slice(64 * b, 64 * b + 64)
                            st = mm(bank[2 + gp][64 * b:64 * b + 64, 256 * g2:256 * g2 + 256],
                                    KS[:, u, 2 * gp + g2, toks], QE[:, u, :, 2 * gp + g2, toks], False, True)
                    st.then_inc(s_st[gp], 1)
                if not (isinstance(t, int) and t == 0):
                    products(t - 1, u + 3)

            attention(pe, lead, follow)
            products(NT - 1, 1)

            pe.wait_ge(s_o, NT)
            for s in range(NQ + 2):
                if s >= 2:
                    q = s - 2
                    pe.wait_ge(s_oh, q + 1)
                    pe.wait_ge(s_pos, q)
                    oh = ohb[:, :, :].rearrange("p t e -> p (t e)")
                    mm(bank[4][:, 0:4 * E], before[:, :], oh, True, True)
                    mm(bank[4][:, 4 * E:8 * E], ones_b[:, :], oh, False, True).then_inc(s_rk, 1)
                if s < NQ:
                    pe.wait_ge(s_otev, s)
                    for j in range(4):
                        tr = pe.transpose(bank[0][:, P * j:P * j + P], O[:, 4 * s + j, :], ident[:, :])
                    tr.then_inc(s_ot, 1)
                    pe.wait_ge(s_otev, s + 1)
                    pe.wait_ge(s_x2, s)
                    for j in range(4):
                        for b in (0, 1):
                            for r in (0, 1):
                                rows = slice(64 * b, 64 * b + 64)
                                op = mm(bank[1][rows, P * j:P * j + P],
                                        OT[rows, s % 2, P * j + 64 * r:P * j + 64 * r + 64], WO[rows, r, :],
                                        j == 0 and r == 0, r == 1)
                    op.then_inc(s_op, 1)
                if 1 <= s <= NQ:
                    q = s - 1
                    pe.wait_ge(s_xn2, q + 1)
                    pe.wait_ge(s_x2ev, q)
                    for j in range(4):
                        tr = pe.transpose(bank[2][:, P * j:P * j + P], XN[:, q % 2, j, :], ident[:, :])
                    tr.then_inc(s_x2t, 1)
                    pe.wait_ge(s_x2ev, q + 1)
                    pe.wait_ge(s_oh, q)
                    for j in range(4):
                        lgm = mm(bank[3][:, E * j:E * j + E], XN2T[:, q % 2, P * j:P * j + P], wr_sb[:, :], j == 0, True)
                    lgm.then_inc(s_lg, 1)

            def rows_in(u, i, done):
                pe.wait_ge(s_xg[u % R6], arrived[u // R6])
                for k in (0, 1):
                    tr = pe.transpose(bank[6][:, :].bitcast(F16)[:, P * k:P * k + P], XG[:, u % R6, P * k:P * k + P],
                                      ident16[:, :])
                tr.then_inc(done, 1)

            arrived = {}

            base = {}

            def load_bases(first, n, turn):
                for ahead in (0, 1):
                    count = 16 * (turn + 1 + ahead)
                    arrived[ahead] = count if isinstance(turn, int) else pe.snap(count)
                _, values = nc.values_load_multi_w_load_instructions(
                    tile_base[0:1, bass.ds(first, n)], engines=(mybir.EngineType.PE,), min_val=0, max_val=(E - 1) * EW,
                    skip_runtime_bounds_check_because="the table holds min(expert, E - 1) * EW")
                base.update(enumerate(values))

            def gate_up(s, u):
                p = u % 2
                pe.wait_ge(s_xtev, s + 1)
                for n, (half, w) in enumerate(((0, 0), (0, 1), (1, 0))):
                    for gu in (0, 1):
                        g = mm(bank[2 * gu + p][:, :], XGT[:, p, half, :],
                               WE[:, bass.ds(base[u] + (2 * H * w + H * gu), H)], n == 0, n == 2)
                g.then_inc(s_gu, 1)

            def hidden_rows(s, u):
                p = u % 2
                pe.wait_ge(s_hl, s + 2)
                for k in (0, 1):
                    for hc in range(HC):
                        at = H * k + P * hc
                        tr = pe.transpose(bank[4 + p][:, :].bitcast(F16)[:, at:at + P], HH[:, p, k, P * hc:P * hc + P],
                                          ident16[:, :])
                tr.then_inc(s_ht, 1)

            def down(s, u):
                p = u % 2
                pe.wait_ge(s_htev, s + 3)
                for hc in range(HC):
                    at = base[u] + (4 * H + 2 * D * hc)
                    mm(bank[7][:, 0:256], HT[:, p, 0, P * hc:P * hc + P], WE[:, bass.ds(at, 2 * D)], hc == 0)
                    y = mm(bank[7][:, 0:P], HT[:, p, 1, P * hc:P * hc + P], WE[:, bass.ds(at, D)], False, hc == HC - 1)
                y.then_inc(s_y, 1)

            def ffn_step(s, u, i, gu, th, dn):
                if gu:
                    gate_up(s, u)
                if gu and gu != "last":
                    rows_in(u + 1, i, s_xt)
                if th:
                    hidden_rows(s - 1, u - 1)
                if dn and not th:
                    pe.wait_ge(s_yev, FT - 1)
                if dn:
                    down(s - 2, u - 2)

            pe.wait_ge(s_table, 2)
            for par in (0, 1):
                pe.wait_ge(s_wl[par], E // 2)
            arrived[0] = 16
            rows_in(0, 0, s_xt0)
            experts(pe, ffn_step, load_bases)

        @block.vector
        def _(dve):
            step = Chain(dve, s_dve)
            for s_ring, n in ((s_hl, 1), (s_ht, 1), (s_htev, 2), (s_y, 2), (s_yt, 2)):
                dve.sem_inc(s_ring, n)
            dve.memset(ones_f[:, :], 1.0)
            dve.memset(QE[:, :, :, :, :].rearrange("p a r g t -> p (a r g t)").bitcast(F32), 0.0).then_inc(s_dconsts, 1)
            dve.memset(KS[:, :, :, :].rearrange("p a g t -> p (a g t)").bitcast(F32), 0.0).then_inc(s_dconsts, 1)
            dve.memset(runs[:, :], 0.0)
            dve.wait_ge(s_dconsts, 2)

            def norm_stats(src, t, ready):
                for j in range(4):
                    last = dve.bn_stats(stats[:, j, :], src[:, 4 * t + j, :])
                step(last)
                for j in range(4):
                    last = dve.bn_aggr(mv[:, j, :], stats[:, j, :])
                step(last)
                dve.tensor_scalar(ve[:, :], mv[:, :, 1], EPS, None, ALU.add).then_inc(ready, 1)

            def norm_apply(src, t, estimate, done):
                dve.wait_ge(estimate, t + 1)
                step(dve.tensor_tensor(nt[:, :], r0[:, :], r0[:, :], ALU.mult))
                step(dve.tensor_tensor(nt[:, :], nt[:, :], ve[:, :], ALU.mult))
                step(dve.tensor_scalar(nt[:, :], nt[:, :], -0.5, 1.5, ALU.mult, ALU.add))
                step(dve.tensor_tensor(nt[:, :], nt[:, :], r0[:, :], ALU.mult))
                for j in range(4):
                    last = dve.tensor_scalar(XN[:, t % 2, j, :], src[:, 4 * t + j, :], mv[:, j, 0:1], nt[:, j:j + 1],
                                             ALU.subtract, ALU.mult)
                last.then_inc(done, 1)

            def norm(t):
                dve.wait_ge(s_x[t % 2], 32 * (t // 2 + 1))
                norm_stats(X, t, s_var)
                norm_apply(X, t, s_rs, s_xn)

            dve.wait_ge(s_weights, 16 * N_W)
            for r in (0, 1):
                for dup in (0, 1):
                    last = dve.tensor_copy(woP[:, r, 64 * dup:64 * dup + 64].rearrange("o (g d) -> o g d", d=HD),
                                           w_nat[:, 3, :].rearrange("o (g r d) -> o r g d", r=2, d=HD)[:, r])
            last.then_inc(s_wperm, 1)
            dve.tensor_scalar(bqs_c[:, :], bq_c[:, :], SCALE, None, ALU.mult)
            dve.tensor_scalar(bvb[:, :], ones_f[:, :], bv_c[:, 0:1], None, ALU.mult).then_inc(s_wperm, 1)
            dve.wait_ge(s_wt, 3)
            dve.tensor_tensor(bias_row[:, :], bank[5][:, 0:P], bo_b[:, :], ALU.add).then_inc(s_bias, 1)

            def low(t):
                par = t % 2
                for n, bias in enumerate((bqs_c, bk_c)):
                    dve.wait_ge(s_hi, 3 * t + n + 1)
                    dve.scalar_tensor_tensor(out=QK[:, par, n, 1, :], in0=bank[2 + 2 * n + par][:, :],
                                             scalar=bias[:, 0:1], in1=QK[:, par, n, 0, :],
                                             op0=ALU.add, op1=ALU.subtract).then_inc(s_lo, 1)
                dve.wait_ge(s_hi, 3 * t + 3)
                dve.wait_ge(s_consts, N_CONST)
                for b in (0, 1):
                    rows = slice(64 * b, 64 * b + 64)
                    last = dve.tensor_tensor(VB[rows, 4 * t:4 * t + 4, :, 18 + 9 * b:26 + 9 * b],
                                             bank[6 + par][rows, :].rearrange("p (t h d) -> p t h d", t=4, d=HD),
                                             VB[rows, 4 * t:4 * t + 4, :, 9 * b:9 * b + 8], ALU.subtract)
                last.then_inc(s_lo, 1)

            norm(0)
            norm(1)
            for t in range(NQ):
                low(t)
                if t + 2 < NQ:
                    norm(t + 2)

            def lead(t, u, i):
                for b in (0, 1):
                    dve.wait_ge(s_sc[b], t + 1)
                    last = dve.tensor_reduce(MX[:, u % 2, :, b], bank[b][:, :].rearrange("p (v k) -> p v k", k=64),
                                             AX.X, ALU.max)
                last.then_inc(s_max, 1)

            Ot = O[:, :, :].rearrange("p t n -> p (t n)")

            def normalise(t, u):
                dve.wait_ge(s_pv, t + 1)
                pv = bank[4 + u % 2][:, 0:288].rearrange("p (v w) -> p v w", w=36)
                step(dve.tensor_copy(SM[:, :, :], pv[:, :, 18:36]))
                step(dve.tensor_tensor(SM[:, :, :], pv[:, :, 0:18], SM[:, :, :], ALU.add))
                sm = SM[:, :, :].rearrange("p v (b w) -> p v b w", b=2)
                step(dve.reciprocal(RS[:, :, :], sm[:, :, :, 8]))
                dve.tensor_tensor(Ot[:, bass.ds(t * P, P)].rearrange("p (b v d) -> p v b d", b=2, d=HD),
                                  sm[:, :, :, 0:8], RS[:, :, :].unsqueeze(3).to_broadcast([P, 8, 2, HD]),
                                  ALU.mult).then_inc(s_o, 1)

            def follow(t, u, i):
                for gp in (0, 1):
                    half = slice(512 * gp, 512 * gp + 512)
                    dve.wait_ge(s_ph[gp], t + 1)
                    dve.tensor_tensor(PL[:, u % 2, half], P32[:, gp, :], PH[:, u % 2, half], ALU.subtract).then_inc(s_pl[gp], 1)
                if not (isinstance(t, int) and t == 0):
                    if not (isinstance(t, int) and t == 1):
                        dve.wait_ge(s_o, t - 1)
                    normalise(t - 1, u + 3)

            attention(LoopChain(dve, step, 12, 2), lead, follow)
            dve.wait_ge(s_o, NT - 1)
            normalise(NT - 1, 1)

            dve.wait_ge(s_tanh, 1)
            step(dve.tensor_scalar(bias_row[:, :], bias_row[:, :], tg[:, 0:1], None, ALU.mult))
            step(dve.tensor_tensor(X[:, :, :], X[:, :, :], bias_row[:, :].unsqueeze(1).to_broadcast([P, NT, D]), ALU.add))
            dve.tensor_copy(jrow[:, :], jint[:, :])
            dve.tensor_scalar(tie[:, :], eint[:, :], -1.0, float(E), ALU.mult, ALU.add)
            step(dve.tensor_scalar(ebase[:, :], eint[:, :], float(N), None, ALU.mult))

            def first_of(oh, vals, top):
                b = lambda v: v[:, :].unsqueeze(2).to_broadcast([P, 4, E])
                step(dve.tensor_reduce(top[:, :], vals[:, :, :], AX.X, ALU.max))
                step(dve.tensor_tensor(oh[:, :, :], vals[:, :, :], b(top), ALU.is_equal))
                step(dve.tensor_tensor(oh[:, :, :], oh[:, :, :], tie[:, :].unsqueeze(1).to_broadcast([P, 4, E]), ALU.mult))
                step(dve.tensor_reduce(tm[:, :], oh[:, :, :], AX.X, ALU.max))
                step(dve.tensor_tensor(oh[:, :, :], oh[:, :, :], b(tm), ALU.is_equal))

            oh1s, oh2s = [oh1, oh1b], [oh2, oh2b]
            for s in range(NQ + 2):
                if s >= 2:
                    q = s - 2
                    par = q % 2
                    dve.wait_ge(s_rk, q + 1)
                    for j in range(4):
                        step(dve.tensor_tensor(rank[:, j, :], bank[4][:, E * j:E * j + E], runs[:, :], ALU.add))
                        step(dve.tensor_tensor(runs[:, :], runs[:, :], bank[4][:, 4 * E + E * j:4 * E + E * j + E], ALU.add))
                    step(dve.tensor_tensor(rank[:, :, :], rank[:, :, :], ebase[:, :].unsqueeze(1).to_broadcast([P, 4, E]),
                                           ALU.add))
                    for k, o in enumerate((oh1s[par], oh2s[par])):
                        step(dve.tensor_tensor(le[:, :, :], o[:, :, :], rank[:, :, :], ALU.mult))
                        step(dve.tensor_reduce(posf[:, k, :], le[:, :, :], AX.X, ALU.add))
                    if q >= 2:
                        dve.wait_ge(s_sent[par], 128)
                    dve.tensor_copy(pos[:, par, :, :], posf[:, :, :]).then_inc(s_pos, 1)
                if s < NQ:
                    t4 = slice(4 * s, 4 * s + 4)
                    dve.wait_ge(s_op, s + 1)
                    dve.scalar_tensor_tensor(out=X2[:, t4, :], in0=bank[1][:, :].rearrange("p (t n) -> p t n", n=D),
                                             scalar=tg[:, 0:1], in1=X[:, t4, :], op0=ALU.mult, op1=ALU.add)\
                       .then_inc(s_x2, 1)
                    dve.wait_ge(s_x2, s + 1)
                    norm_stats(X2, s, s_rv)
                    norm_apply(X2, s, s_rrs, s_xn2)
                    dve.wait_ge(s_xn2, s + 1)
                    par = s % 2
                    if s >= 2:
                        dve.wait_ge(s_sent[par], 128)
                    step(dve.tensor_copy(XHL[:, par, 0, :, 0:D], XN[:, par, :, :]))
                    step(dve.tensor_tensor(XHL[:, par, 0, :, D:2 * D], XN[:, par, :, :], XHL[:, par, 0, :, 0:D], ALU.subtract))
                    dve.tensor_copy(XHL[:, par, 1, :, 0:2 * D], XHL[:, par, 0, :, 0:2 * D])
                    for k in range(K):
                        last = dve.tensor_copy(XHL[:, par, k, :, 2 * D:XW].bitcast(I32), ids[:, t4, k:k + 1])
                    step(last)
                if 1 <= s <= NQ:
                    q = s - 1
                    o1, o2 = oh1s[q % 2], oh2s[q % 2]
                    dve.wait_ge(s_lg, q + 1)
                    step(dve.tensor_tensor(lg[:, :, :], bank[3][:, 0:4 * E].rearrange("p (t e) -> p t e", e=E),
                                           br_b[:, :].unsqueeze(1).to_broadcast([P, 4, E]), ALU.add))
                    first_of(o1, lg, m1)
                    step(dve.scalar_tensor_tensor(out=le[:, :, :], in0=o1[:, :, :], scalar=NEG, in1=lg[:, :, :],
                                                  op0=ALU.mult, op1=ALU.add))
                    first_of(o2, le, m2)
                    if q >= 1:
                        dve.wait_ge(s_rk, q)
                    dve.tensor_tensor(ohb[:, :, :], o1[:, :, :], o2[:, :, :], ALU.add).then_inc(s_oh, 1)
                    dve.tensor_tensor(m2[:, :], m2[:, :], m1[:, :], ALU.subtract).then_inc(s_gin, 1)
                    dve.wait_ge(s_gexp, q + 1)
                    step(dve.tensor_scalar(m1[:, :], m2[:, :], 1.0, None, ALU.add))
                    step(dve.reciprocal(m1[:, :], m1[:, :]))
                    t4 = slice(4 * q, 4 * q + 4)
                    step(dve.tensor_scalar(gw[:, t4, 0], m1[:, :], tg[:, 1:2], None, ALU.mult))
                    step(dve.tensor_tensor(gw[:, t4, 1], m2[:, :], gw[:, t4, 0], ALU.mult))

            one = lambda v: v[0:1, :]
            step(dve.tensor_scalar(cnt_i[:, :], one(runs), float(P - 1), None, ALU.add))
            step(dve.tensor_scalar(cnt_i[:, :], cnt_i[:, :], 7, None, ALU.logical_shift_right))
            step(dve.tensor_copy(cnt_f[:, :], cnt_i[:, :]))
            step(dve.tensor_tensor_scan(tiles_to[:, :], ones_f[0:1, 0:E], cnt_f[:, :], 0.0, ALU.mult, ALU.add))
            jb = jrow[:, :].unsqueeze(2).to_broadcast([1, FT, E])
            eb = lambda v: v[:, :].unsqueeze(1).to_broadcast([1, FT, E])
            step(dve.tensor_tensor(jge[:, :, :], jb, eb(tiles_to), ALU.is_ge))
            step(dve.tensor_reduce(jex[:, :], jge[:, :, :], AX.X, ALU.add))
            step(dve.tensor_tensor(jge[:, :, :], jge[:, :, :], eb(cnt_f), ALU.mult))
            step(dve.tensor_reduce(jbk[:, :], jge[:, :, :], AX.X, ALU.add))
            step(dve.tensor_tensor(jbk[:, :], jrow[:, :], jbk[:, :], ALU.subtract))
            step(dve.tensor_scalar(jbk[:, :], jbk[:, :], float(P), None, ALU.mult))
            dve.scalar_tensor_tensor(out=tile_row[:, 0:FT], in0=jex[:, :], scalar=float(N), in1=jbk[:, :],
                                     op0=ALU.mult, op1=ALU.add).then_inc(s_table, 1)
            dve.tensor_scalar(tile_base[:, 0:FT], jex[:, :], float(E - 1), float(EW), ALU.min, ALU.mult).then_inc(s_table, 1)

            def rows_out(u):
                dve.tensor_copy(XGT[:, u % 2, :, :].rearrange("p k n -> p (k n)"), bank[6][:, :].bitcast(F16)[:, 0:256])\
                   .then_inc(s_xtev, 1)

            def ffn_step(s, u, i, gu, th, dn):
                p = u % 2
                if gu and gu != "last":
                    dve.wait_ge(s_xt, s + 1)
                    rows_out(u + 1)
                if gu:
                    dve.wait_ge(s_silu, s + 1)
                    dve.tensor_tensor(HF[:, p, :], SG[:, p, :], bank[2 + p][:, :], ALU.mult).then_inc(s_h, 1)
                if dn:
                    dve.wait_ge(s_y, s + 1)
                    dve.tensor_copy(YT[:, u % 2, :], bank[7][:, P:2 * P]).then_inc(s_yt, 1)
                    dve.wait_ge(s_yt, s + 1)
                    dve.tensor_tensor(YS[:, (u - 2) % R6, :], bank[7][:, 0:P], YT[:, u % 2, :], ALU.add).then_inc(s_yev, 1)
                if gu:
                    dve.wait_ge(s_hh, s + 1)
                    dve.tensor_tensor(HH[:, p, 1, :], HF[:, p, :], HH[:, p, 0, :], ALU.subtract).then_inc(s_hl, 1)

            dve.wait_ge(s_xt0, 1)
            rows_out(0)
            experts(dve, ffn_step)

            for q in range(NQ):
                dve.wait_ge(s_ya[q], 16)
                for k in range(K):
                    for j in range(4):
                        t = 4 * q + j
                        last = dve.scalar_tensor_tensor(out=X2[:, t, :], in0=YAk[q % 2][:, j, k, :],
                                                        scalar=gw[:, t, k:k + 1], in1=X2[:, t, :],
                                                        op0=ALU.mult, op1=ALU.add)
                    if k == 0:
                        step(last)
                last.then_inc(s_fin, 1)


_INS = ['x', 'ctx_1024', 'g_xattn', 'g_ffn', 'L0_xattn_wq', 'L0_xattn_bq', 'L0_xattn_wk', 'L0_xattn_bk', 'L0_xattn_wv',
        'L0_xattn_bv', 'L0_xattn_wo', 'L0_xattn_bo', 'L0_ffn_Wr', 'L0_ffn_br', 'L0_ffn_Wg', 'L0_ffn_Wu', 'L0_ffn_Wd']


def kernel(**inputs):
    import numpy as _np
    import concourse.bacc as _bacc
    from concourse import mybir as _mybir
    from concourse.bass_utils import run_bass_kernel_spmd as _run

    nc = _bacc.Bacc("TRN2", target_bir_lowering=False, num_devices=1)
    arrays, args = {}, []
    for name in _INS:
        a = _np.ascontiguousarray(inputs[name])
        arrays[f"in_{name}_dram"] = a
        args.append(nc.dram_tensor(f"in_{name}_dram", a.shape, _mybir.dt.from_np(a.dtype), kind="ExternalInput").ap())
    shape = inputs["x"].shape
    out = nc.dram_tensor("out_0_dram", shape, _mybir.dt.float32, kind="ExternalOutput").ap()
    flamingo_gated_block(nc, *args, out)
    r = _run(nc, [arrays], core_ids=[0])
    return r.results[0]["out_0_dram"]
```

```python
from contextlib import ExitStack, contextmanager

import concourse.bass as bass
from concourse import mybir

ALU = mybir.AluOpType
ACT = mybir.ActivationFunctionType
AX = mybir.AxisListType
F32 = mybir.dt.float32
F16 = mybir.dt.float16
BF16 = mybir.dt.bfloat16
I32 = mybir.dt.int32

P = 128
NEG = -1.0e30
EPS = 1.0e-5


class LoopChain:

    def __init__(self, eng, chain, steps, turns):
        self.eng, self.chain, self.steps, self.turns = eng, chain, steps, turns
        self.snap = eng.snap

    @contextmanager
    def Fori(self, start, end):
        with self.eng.Fori(start, end) as i:
            self.chain.turn(i - start, self.steps)
            yield i
        self.chain.end(self.turns)


class Chain:

    def __init__(self, eng, sem):
        self.eng, self.sem, self.base, self.n, self.steps = eng, sem, 0, 0, 0

    def __call__(self, instruction):
        instruction.then_inc(self.sem, 1)
        self.n += 1
        self.eng.wait_ge(self.sem, self.base + self.n)

    def turn(self, i, steps):
        self.start, self.steps = self.n, steps
        self.base = self.eng.snap(i * steps)

    def end(self, turns):
        assert self.n - self.start == self.steps, (self.n - self.start, self.steps)
        self.base, self.n = 0, self.start + self.steps * turns


def flamingo_gated_block(nc, x, ctx_in, g_xattn, g_ffn, wq, bq, wk, bk, wv, bv, wo, bo, Wr, br, Wg, Wu, Wd, out):
    B, T, D = x.shape
    E, _, H = Wg.shape
    HEADS = 16
    HD = D // HEADS
    SCALE = HD ** -0.5
    N = B * T
    NT = N // P
    NQ = NT // 4
    RS4 = 4
    HC = H // P
    K = 2
    FT = (N * K) // P + E - 1
    TRASH = E * N
    XROWS = TRASH + (FT - N * K // P) * P
    R6 = 6
    XW = 2 * D + 2
    assert (T, D, HD, HC, NQ, E, FT) == (64, P, 8, 4, 4, 8, 39)

    x_t = x.rearrange("(t b) q c -> (b q) t c", b=2)
    c_t = ctx_in.rearrange("(t b) q c -> (b q) t c", b=2)
    out_t = out.rearrange("(t b) q c -> (b q) t c", b=2)

    with ExitStack() as ctx:
        def sb(name, shape, dt):
            return ctx.enter_context(nc.sbuf_tensor(name, shape, dt))

        def sem(name):
            return ctx.enter_context(nc.semaphore(name))

        def dram(name, shape, dt):
            return nc.dram_tensor(name, shape, dt, kind="Internal").ap()

        parts = dram("parts", [NT, 6, P, P], F16)
        routed = dram("routed", [XROWS, XW], F16)
        expert_out = dram("expert_out", [N * K, D], F32)

        X = sb("X", [P, NT, D], F32)
        C = sb("C", [P, NT, D], F32)
        XN = sb("XN", [P, 2, 4, D], F32)
        xT = sb("xT", [P, 2, 512], F32)
        cT = sb("cT", [P, 2, 512], F32)
        QKX = sb("QKX", [P, 2 * K * 4 * XW], F16)
        QK = QKX[:, 0:4096].rearrange("p (a n h t) -> p a n h t", a=2, n=2, h=2)
        w_nat = sb("w_nat", [P, 4, D], F32)
        wqT = sb("wqT", [P, D], F32)
        wkT = sb("wkT", [P, D], F32)
        wvT = sb("wvT", [P, D], F32)
        woT = sb("woT", [P, D], F32)
        woP = sb("woP", [P, P], F32)
        WO = sb("WO", [P, D], F32)
        b_nat = sb("b_nat", [1, 2, P], F32)
        b_row = sb("b_row", [1, 2, P], F32)
        b_col = sb("b_col", [P, 2], F32)
        bv_c = sb("bv_c", [P, 1], F32)
        bvb = sb("bvb", [P, P], F32)
        bo_b = sb("bo_b", [P, D], F32)
        bias_row = sb("bias_row", [P, D], F32)
        br_b = sb("br_b", [P, E], F32)
        wr_sb = sb("wr_sb", [P, E], F32)
        gx = sb("gx", [P, 2], F32)
        tg = sb("tg", [P, 2], F32)
        ident = sb("ident", [P, P], F32)
        ident16 = sb("ident16", [P, P], F16)
        identb = sb("identb", [P, P], BF16)
        ones_f = sb("ones_f", [P, P], F32)
        mask_q = sb("mask_q", [P, 64], BF16)
        shift_w = sb("shift_w", [80, 8, P], BF16)
        shift_m = sb("shift_m", [80, 2, P], BF16)
        before = sb("before", [P, P], BF16)
        ones_b = sb("ones_b", [P, P], BF16)
        QE = sb("QE", [P, RS4, 8, 4, 64], F16)
        KS = sb("KS", [P, RS4, 4, P], F16)
        VB = sb("VB", [P, NT, HEADS, 36], F16)
        VW = HEADS * 36
        VR = sb("VR", [P, 4, VW], F16)
        VBf = VB[:, :, :, :].rearrange("p t h w -> p (t h w)")
        MX = sb("MX", [P, 2, 8, 2], F32)
        P32 = sb("P32", [P, 2, 512], F32)
        PH = sb("PH", [P, 2, 1024], F16)
        PL = sb("PL", [P, 2, 1024], F16)
        SM = sb("SM", [P, 8, 18], F32)
        RS = sb("RS", [P, 8, 2], F32)
        YA = VB[:, :, :, :].rearrange("p t h w -> p (t h w)")[:, 0:NT * K * D * 2].bitcast(F32)\
            .rearrange("p (t n) -> p t n", t=NT)
        stats = sb("stats", [P, NT, 6], F32)
        mv = sb("mv", [P, NT, 2], F32)
        ve = sb("ve", [P, NT], F32)
        lnv = sb("lnv", [P, NT], F32)
        r0 = sb("r0", [P, NT], F32)
        nt = sb("nt", [P, NT], F32)
        X2 = C
        O = sb("O", [P, 2, D], F32)
        OT = xT[:, 0, 0:2 * P].rearrange("p (a n) -> p a n", a=2)
        XN2 = X
        XN2T = cT
        XHLa = sb("XHL", [P, 2, K, 4, XW], F16)
        XHLb = QKX[:, :].rearrange("p (a k t w) -> p a k t w", a=2, k=K, t=4)
        XHL = [XHLa[:, 0], XHLa[:, 1], XHLb[:, 0], XHLb[:, 1]]
        lg = sb("lg", [P, NT, E], F32)
        le = sb("le", [P, NT, E], F32)
        tie = sb("tie", [P, E], F32)
        ebase = sb("ebase", [P, E], F32)
        m1 = sb("m1", [P, NT], F32)
        m2 = sb("m2", [P, NT], F32)
        tm = sb("tm", [P, NT], F32)
        oh1 = sb("oh1", [P, NT, E], F32)
        oh2 = sb("oh2", [P, NT, E], F32)
        ohb = sb("ohb", [P, NT, E], BF16)
        rank = sb("rank", [P, NT, E], F32)
        posf = sb("posf", [P, K, NT], F32)
        pos = sb("pos", [P, K, NT], I32)
        runs = sb("runs", [P, E], F32)
        gw = sb("gw", [P, NT, K], F32)
        cnt_i = sb("cnt_i", [1, E], I32)
        cnt_f = sb("cnt_f", [1, E], F32)
        tiles_to = sb("tiles_to", [1, E], F32)
        eint = sb("eint", [P, E], I32)
        jint = sb("jint", [1, FT], I32)
        jrow = sb("jrow", [1, FT], F32)
        jge = sb("jge", [1, FT, E], F32)
        jex = sb("jex", [1, FT], F32)
        jbk = sb("jbk", [1, FT], F32)
        tile_row = sb("tile_row", [1, FT + 1], I32)
        tile_base = sb("tile_base", [1, FT + 9], I32)
        fill = sb("fill", [P, XW], F16)
        WS = sb("WS", [P, 2, 3, 512], F32)
        EW = 4 * H + 2 * D * HC
        WE = sb("WE", [P, E * EW], F16)

        XG = sb("XG", [P, R6, XW], F16)
        XGT = sb("XGT", [P, 2, 2, P], F16)
        QEf = QE[:, :, :, :, :].rearrange("p a r g t -> p (a r g t)").bitcast(F32)
        SG = QEf[:, 0:2 * H].rearrange("p (a n) -> p a n", a=2)
        HF = QEf[:, 2 * H:4 * H].rearrange("p (a n) -> p a n", a=2)
        HH = sb("HH", [P, 2, 2, H], F16)
        HT = sb("HT", [P, 2, 2, H], F16)
        YS = sb("YS", [P, R6, D], F32)
        bank = [ctx.enter_context(nc.psum_tensor(f"bank{i}", [P, 512], F32)) for i in range(8)]


        def down_half(e, k):
            w = WE[:, bass.ds(e * EW + 4 * H, 2 * D * HC)]
            return w.rearrange("p (h k n) -> p k h n", h=HC, k=2)[:, k]

        parts_k = parts[:, 0:4].rearrange("t c (d r g) k -> t r (c d) (g k)", r=4, g=4)
        parts_q = parts[:, 3:6].rearrange("t c (d r g) k -> t r (c d) (g k)", r=4, g=4)

        s_weights = sem("s_weights")
        s_x = [sem(f"s_x_in{i}") for i in range(NQ)]
        s_c = [sem(f"s_c_in{i}") for i in range(NQ)]
        s_pool = sem("s_pool")
        s_turns = sem("s_turns")
        s_consts = sem("s_consts")
        s_ids = sem("s_ids")
        s_dconsts = sem("s_dconsts")
        s_fill = sem("s_fill")
        s_wt = sem("s_wt")
        s_wev = sem("s_wev")
        s_wperm = sem("s_wperm")
        s_tanh = sem("s_tanh")
        s_bias = sem("s_bias")
        s_dve = sem("s_dve")
        s_act = sem("s_act")
        s_var = sem("s_var")
        s_rs = sem("s_rs")
        s_xn = sem("s_xn")
        s_tr = sem("s_tr")
        s_trev = sem("s_trev")
        s_qkv = sem("s_qkv")
        s_hi = sem("s_hi")
        s_lo = sem("s_lo")
        s_parts = [sem("s_parts0"), sem("s_parts1")]
        s_stack = [sem(f"s_stack{i}") for i in range(RS4)]
        s_sc = [sem("s_sc0"), sem("s_sc1")]
        s_max = sem("s_max")
        s_mt = sem("s_mt")
        s_shift = sem("s_shift")
        s_st = [sem("s_st0"), sem("s_st1")]
        s_exp = [sem("s_exp0"), sem("s_exp1")]
        s_ph = [sem("s_ph0"), sem("s_ph1")]
        s_pl = [sem("s_pl0"), sem("s_pl1")]
        s_pv = sem("s_pv")
        s_o = sem("s_o")
        s_ws = [sem("s_ws0"), sem("s_ws1")]
        s_wh = [sem("s_wh0"), sem("s_wh1")]
        s_wl = [sem("s_wl0"), sem("s_wl1")]
        s_ot = sem("s_ot")
        s_otev = sem("s_otev")
        s_op = sem("s_op")
        s_x2 = sem("s_x2")
        s_stats = sem("s_stats")
        s_rv = sem("s_rv")
        s_rrs = sem("s_rrs")
        s_xn2 = sem("s_xn2")
        s_x2t = sem("s_x2t")
        s_x2ev = sem("s_x2ev")
        s_lg = sem("s_lg")
        s_oh = sem("s_oh")
        s_gin = sem("s_gin")
        s_gexp = sem("s_gexp")
        s_rk = sem("s_rk")
        s_xhl = sem("s_xhl")
        s_pos = sem("s_pos")
        s_sent = sem("s_sent")
        s_table = sem("s_table")
        s_xg = [sem(f"s_xg{i}") for i in range(R6)]
        s_xt = sem("s_xt")
        s_xt0 = sem("s_xt0")
        s_xtev = sem("s_xtev")
        s_gu = sem("s_gu")
        s_silu = sem("s_silu")
        s_h = sem("s_h")
        s_hh = sem("s_hh")
        s_hl = sem("s_hl")
        s_ht = sem("s_ht")
        s_htev = sem("s_htev")
        s_y = sem("s_y")
        s_yev = sem("s_yev")
        s_ysent = [sem(f"s_ysent{i}") for i in range(R6)]
        s_ya = [sem(f"s_ya{i}") for i in range(4)]
        s_pool_sum = sem("s_pool_sum")
        s_weighed = sem("s_weighed")
        s_fin = sem("s_fin")
        s_fin_pool = sem("s_fin_pool")
        s_out = sem("s_out")

        N_CONST = 14
        BATCHES = ((0, 1), (2, 3))
        N_W = 4 + 2 + 6
        block = ctx.enter_context(nc.Block())

        def experts(eng, ffn_step, bases=None):
            load = bases or (lambda first, n, turn: None)
            load(0, 2, 0)
            ffn_step(0, 0, 0, True, False, False)
            ffn_step(1, 1, 0, True, True, False)
            with eng.Fori(0, R6) as turn:
                i = eng.snap(turn * R6)
                load(i, R6 + 2, turn)
                for u in range(2, 2 + R6):
                    ffn_step(i + u, u, i, True, True, True)
            load(FT - 3, 3, R6)
            ffn_step(FT - 1, 2, R6 * R6, "last", True, True)
            ffn_step(FT, 3, R6 * R6, False, True, True)
            ffn_step(FT + 1, 4, R6 * R6, False, False, True)

        def attention(eng, lead, follow):
            def steps(t0, i):
                for u in range(4):
                    if not isinstance(t0, int) or t0 + u + 2 < NT:
                        lead(t0 + u + 2, (u + 2) % 4, i + (u + 2) // 4)
                    follow(t0 + u, u, i)

            lead(0, 0, 0)
            lead(1, 1, 0)
            steps(0, 0)
            with eng.Fori(1, NQ - 1) as i:
                steps(eng.snap(4 * i), i)
            steps(NT - 4, NQ - 1)

        def load_expert(eng, e, par):
            eng.dma_start(WS[:, par, 0, :], Wg[bass.ds(e, 1)].rearrange("o d h -> (o d) h")).then_inc(s_ws[par], 16)
            eng.dma_start(WS[:, par, 1, :], Wu[bass.ds(e, 1)].rearrange("o d h -> (o d) h")).then_inc(s_ws[par], 16)
            eng.dma_start(WS[:, par, 2, :].rearrange("p (c n) -> p c n", c=HC),
                          Wd[bass.ds(e, 1)].rearrange("o (c p) n -> p (o c) n", p=P)).then_inc(s_ws[par], 16)

        OCOL = 288
        xt_bank = [bank[7], bank[7], bank[0], bank[1]]
        lg_bank = [bank[7], bank[2]]
        rk_bank = [bank[7], bank[3]]
        RKC = [8 * E, 0]

        def tiles(quarters):
            return slice(4 * quarters[0], 4 * quarters[-1] + 4)


        @block.sync
        def _(sp):
            for n, w in enumerate((wq, wk, wv, wo)):
                sp.dma_start(w_nat[:, n, :], w).then_inc(s_weights, 16)
            for t in range(NQ):
                sp.dma_start(X[:, 4 * t:4 * t + 4, :], x_t[:, 4 * t:4 * t + 4, :]).then_inc(s_x[t], 16)
            for t in range(NQ):
                sp.dma_start(C[:, 4 * t:4 * t + 4, :], c_t[:, 4 * t:4 * t + 4, :]).then_inc(s_c[t], 16)

            def write_parts(t, par):
                sp.wait_ge(s_lo, 3 * t + 2)
                for c, (q_half, k_half) in enumerate(((0, 0), (0, 1), (1, 0))):
                    for n, half in enumerate((q_half, k_half)):
                        sp.dma_start(parts[4 * t:4 * t + 4, 3 * (1 - n) + c].rearrange("t p k -> p t k"),
                                     QK[:, par, n, half, :].rearrange("p (t k) -> p t k", t=4)).then_inc(s_parts[par], 16)

            def load_stack(t, u):
                for r in range(4):
                    rows = slice(32 * r, 32 * r + 24)
                    sp.dma_start(QE[rows, u, :, r, :],
                                 parts_q[bass.ds(t, 1), r].rearrange("t p (a q) -> (t p) a q", q=64)).then_inc(s_stack[u], 16)
                sp.dma_start(KS[:, u, :, :].rearrange("p g k -> p (g k)"),
                             parts_k[bass.ds(t, 1)].rearrange("t r p k -> (t r) p k")).then_inc(s_stack[u], 16)

            sp.wait_ge(s_dconsts, 3)
            write_parts(0, 0)
            sp.wait_ge(s_parts[0], 96)
            for u in range(RS4):
                load_stack(u, u)
                if u + 1 < NQ:
                    write_parts(u + 1, (u + 1) % 2)
            for p_ in (0, 1):
                sp.wait_ge(s_parts[p_], 2 * 96)
            sp.wait_ge(s_consts, N_CONST)
            r_fill = routed.rearrange("(n p m) w -> n p m w", p=P, m=15)

            def fill_rows(n):
                sp.dma_start(r_fill[bass.ds(n, 1)].rearrange("o p m w -> (o p) m w"),
                             fill[:, :].unsqueeze(1).to_broadcast([P, 15, XW])).then_inc(s_fill, 16)

            with sp.Fori(0, NQ - 1) as i:
                for u in range(RS4):
                    sp.wait_ge(s_st[1], 4 * i + u + 1)
                    load_stack(4 * i + u + 4, u)
                    if u < 3:
                        fill_rows(3 * i + u)

            sp.wait_ge(s_fill, 16 * r_fill.shape[0])
            sp.wait_ge(s_sent, 16 * K * NT)
            sp.wait_ge(s_table, 2)

            def load_rows(j, u):
                row = sp.value_load(tile_row[0:1, bass.ds(j, 1)], min_val=0, max_val=XROWS - P)
                sp.dma_start(XG[:, u, :], routed[bass.ds(row, P), :]).then_inc(s_xg[u], 16)

            for j in range(R6):
                load_rows(j, j)
            with sp.Fori(1, 6) as i:
                for u in range(R6):
                    sp.wait_ge(s_ysent[u], i * 16)
                    load_rows(R6 * i + u, u)
            for u in range(FT - 6 * R6):
                sp.wait_ge(s_ysent[u], 6 * 16)
                load_rows(6 * R6 + u, u)
            for u in range(R6):
                sp.wait_ge(s_ysent[u], 16 * (7 if u < FT - 6 * R6 else 6))
            r_out = expert_out[0:N * K, :].rearrange("(t p k) n -> p t (k n)", p=P, k=K)
            for q in (0, 3, 1, 2):
                sp.dma_start(YA[:, 4 * q:4 * q + 4, :], r_out[:, 4 * q:4 * q + 4, :]).then_inc(s_ya[q], 16)
            for q in (0, 1, 3, 2):
                if q == NQ - 1:
                    sp.wait_ge(s_fin_pool, 1)
                else:
                    sp.wait_ge(s_fin, q + 1)
                sp.dma_start(out_t[:, 4 * q:4 * q + 4, :], X2[:, 4 * q:4 * q + 4, :]).then_inc(s_out, 16)
            sp.wait_ge(s_out, 16 * NQ)


        @block.gpsimd
        def _(pool):
            const = Chain(pool, s_consts)
            pool.memset(ident[:, :], 0.0).then_inc(s_pool, 1)
            pool.wait_ge(s_pool, 1)

            def diagonal(t):
                const(pool.affine_select(out=t[:, :], in_=t[:, :], compare_op=ALU.not_equal, fill=1.0,
                                         base=0, pattern=[[-1, P]], channel_multiplier=1))

            diagonal(ident)
            pool.memset(VB[:, :, :, :].rearrange("p t h w -> p (t h w)").bitcast(F32), 0.0)
            pool.memset(ident16[:, :], 0.0)
            pool.memset(identb[:, :], 0.0)
            pool.memset(mask_q[:, :], 0.0)
            pool.memset(shift_w[:, :, :], 0.0)
            pool.memset(shift_m[:, :, :], 0.0)
            pool.memset(before[:, :], 1.0)
            pool.memset(ones_b[:, :], 1.0)
            pool.memset(fill[:, :].bitcast(F32), 0.0).then_inc(s_pool, 1)
            pool.wait_ge(s_pool, 2)
            for t in (ident16, identb):
                diagonal(t)
            for r in (0, 1):
                m = mask_q[64 * r:64 * r + 64, :]
                const(pool.affine_select(out=m, in_=m, compare_op=ALU.is_ge, fill=NEG,
                                   base=0, pattern=[[-1, 64]], channel_multiplier=1))
            m = shift_w[0:64, :, :].rearrange("p v (b k) -> p (v b) k", b=2)
            const(pool.affine_select(out=m, in_=m, compare_op=ALU.is_ge, fill=NEG,
                               base=0, pattern=[[0, 16], [-1, 64]], channel_multiplier=1))
            m = shift_w[64:80, :, :].rearrange("p v (b k) -> p v b k", b=2)
            const(pool.affine_select(out=m, in_=m, compare_op=ALU.not_equal, fill=1.0,
                               base=0, pattern=[[-2, 8], [-1, 2], [0, 64]], channel_multiplier=1))
            m = shift_m[0:64, :, :].rearrange("p a (b k) -> p (a b) k", b=2)
            const(pool.affine_select(out=m, in_=m, compare_op=ALU.not_equal, fill=1.0,
                               base=0, pattern=[[0, 4], [-1, 64]], channel_multiplier=1))
            const(pool.affine_select(out=before[:, :], in_=before[:, :], compare_op=ALU.is_gt, fill=0.0,
                               base=0, pattern=[[1, P]], channel_multiplier=-1))
            const(pool.memset(VB[0:64, :, :, 8:9], 1.0))
            const(pool.memset(VB[64:P, :, :, 17:18], 1.0))
            const(pool.iota(eint[:, :], pattern=[[1, E]], channel_multiplier=0))
            const(pool.iota(jint[:, :], pattern=[[1, FT]], channel_multiplier=0))
            const(pool.memset(fill[:, 2 * D:XW].bitcast(I32), N * K))

            def low_halves(i, par):
                e = 2 * i + par
                pool.wait_ge(s_wh[par], i + 1)
                g_hi, u_lo = WE[:, bass.ds(e * EW, 2 * H)], WE[:, bass.ds(e * EW + 2 * H, 2 * H)]
                pool.tensor_tensor(u_lo, WS[:, par, 0:2, :].rearrange("p k n -> p (k n)"), g_hi, ALU.subtract)
                pool.tensor_tensor(down_half(e, 1),
                                   WS[:, par, 2, :].rearrange("p (h n) -> p h n", h=HC),
                                   down_half(e, 0),
                                   ALU.subtract).then_inc(s_wl[par], 1)

            def lead(t, u, i):
                pass

            def follow(t, u, i):
                if u % 2 and not (isinstance(t, int) and t == NT - 1):
                    low_halves(i, u // 2)
                    if not (isinstance(i, int) and i == NQ - 1):
                        pool.wait_ge(s_wl[u // 2], i + 1)
                        load_expert(pool, 2 * i + u // 2 + 2, u // 2)

            load_expert(pool, 0, 0)
            load_expert(pool, 1, 1)
            for p_ in (0, 1):
                pool.wait_ge(s_parts[p_], 2 * 96)
            ids = Chain(pool, s_ids)
            for q in range(NQ):
                ids(pool.iota(XHL[q][:, :, :, 2 * D:XW].bitcast(I32).rearrange("p k t o -> p k (t o)"),
                              pattern=[[1, K], [K * P, 4]], base=4 * K * P * q, channel_multiplier=K))
            attention(pool, lead, follow)

            pool.wait_ge(s_fill, 16 * 9)
            for n, quarters in enumerate(BATCHES):
                pool.wait_ge(s_pos, n + 1)
                for q in quarters:
                    pool.wait_ge(s_xhl, q + 1)
                    for k in range(K):
                        for j in range(4):
                            t = 4 * q + j
                            pool.indirect_dma_start(
                                out=routed[:, :], out_offset=bass.IndirectOffsetOnAxis(ap=pos[:, k, t:t + 1], axis=0),
                                in_=XHL[q][:, k, j, :], in_offset=None).then_inc(s_sent, 16)

            low_halves(NQ - 1, 1)

            last_row = pool.to_reg(N * K - 1)

            def scatter(j, u):
                pool.wait_ge(s_table, 2)
                pool.wait_ge(s_yev, j + 1)
                pool.sem_inc(s_turns, 1)
                pool.indirect_dma_start(
                    out=expert_out[:, :],
                    out_offset=bass.IndirectOffsetOnAxis(ap=XG[:, u, 2 * D:XW].bitcast(I32), axis=0),
                    in_=YS[:, u, :], in_offset=None,
                    bounds_check=last_row, oob_is_err=False).then_inc(s_ysent[u], 16)

            with pool.Fori(0, 6) as i:
                for u in range(R6):
                    scatter(R6 * i + u, u)
            for u in range(FT - 6 * R6):
                scatter(6 * R6 + u, u)

            sums = Chain(pool, s_pool_sum)
            quarter = slice(4 * (NQ - 1), 4 * NQ)
            for k in range(K):
                pool.wait_ge(s_weighed, k + 1)
                last = pool.tensor_tensor(X2[:, quarter, :], X2[:, quarter, :], YA[:, quarter, D * k:D * k + D], ALU.add)
                if k == 0:
                    sums(last)
            last.then_inc(s_fin_pool, 1)

        @block.scalar
        def _(act):
            step = Chain(act, s_act)
            for n, b_dram in enumerate((bq, bk)):
                act.dma_start(b_nat[:, n, :], b_dram.rearrange("(o p) -> o p", o=1)).then_inc(s_weights, 16)
            act.dma_start(bv_c[:, :], bv.rearrange("(p o) -> p o", o=1)).then_inc(s_weights, 16)
            act.dma_start(bo_b[:, :], bo.partition_broadcast(P)).then_inc(s_weights, 16)
            act.dma_start(gx[:, 0:1], g_xattn.partition_broadcast(P)).then_inc(s_weights, 16)
            act.dma_start(gx[:, 1:2], g_ffn.partition_broadcast(P)).then_inc(s_weights, 16)
            act.dma_start(br_b[:, :], br.partition_broadcast(P)).then_inc(s_weights, 16)
            act.dma_start(wr_sb[:, :], Wr).then_inc(s_weights, 16)

            act.wait_ge(s_wt, 1)
            for wT, b, scale in ((wqT, bank[0], SCALE), (wkT, bank[1], 1.0)):
                act.activation(wT[:, :].rearrange("c (d r g) -> c g r d", d=HD, r=4),
                               b[:, 0:P].rearrange("c (g r d) -> c g r d", d=HD, r=4), ACT.Copy, scale=scale)\
                   .then_inc(s_wev, 1)
            act.activation(wvT[:, :], bank[2][:, 0:P], ACT.Copy).then_inc(s_wev, 1)
            act.activation(woT[:, :], bank[3][:, 0:P], ACT.Copy).then_inc(s_wev, 1)
            act.wait_ge(s_wt, 2)
            act.activation(WO[:, :], bank[4][:, 0:P], ACT.Copy).then_inc(s_wev, 1)
            act.wait_ge(s_weights, 16 * N_W)
            act.activation(tg[:, :], gx[:, :], ACT.Tanh).then_inc(s_tanh, 1)

            def rsqrt(v_ready, n, done, ts):
                act.wait_ge(v_ready, n)
                step(act.activation(lnv[:, ts], ve[:, ts], ACT.Ln))
                act.activation(r0[:, ts], lnv[:, ts], ACT.Exp, scale=-0.5).then_inc(done, 1)

            rsqrt(s_var, 1, s_rs, slice(0, NT))
            act.wait_ge(s_bias, 1)
            for t in range(NQ):
                par = t % 2
                act.wait_ge(s_tr, 2 * t + 1)
                act.activation(cT[:, par, :], bank[1][:, :], ACT.Copy).then_inc(s_trev, 1)
                act.wait_ge(s_tr, 2 * t + 2)
                act.activation(xT[:, par, :], bank[0][:, :], ACT.Copy).then_inc(s_trev, 1)
                if t >= 2:
                    act.wait_ge(s_parts[par], 96)
                act.wait_ge(s_qkv, 3 * t + 1)
                act.activation(QK[:, par, 1, 0, :], bank[4 + par][:, :], ACT.Identity, bias=b_col[:, 1:2]).then_inc(s_hi, 1)
                act.wait_ge(s_qkv, 3 * t + 2)
                act.activation(QK[:, par, 0, 0, :], bank[2 + par][:, :], ACT.Identity, bias=b_col[:, 0:1]).then_inc(s_hi, 1)
                act.wait_ge(s_qkv, 3 * t + 3)
                if t == 0:
                    act.wait_ge(s_consts, N_CONST)
                for b in (0, 1):
                    rows = slice(64 * b, 64 * b + 64)
                    v = act.activation(VB[rows, 4 * t:4 * t + 4, :, 9 * b:9 * b + 8],
                                       bank[6 + par][rows, :].rearrange("p (t h d) -> p t h d", t=4, d=HD), ACT.Copy)
                v.then_inc(s_hi, 1)

            def output_out(t, u):
                act.wait_ge(s_ot, t + 1)
                turned = bank[6][0:64, P:3 * P].rearrange("p (b r q) -> p r b q", b=2, r=2)
                for r in (0, 1):
                    last = act.activation(OT[64 * r:64 * r + 64, u % 2, :].rearrange("p (b q) -> p b q", b=2),
                                          turned[:, r], ACT.Copy)
                last.then_inc(s_otev, 1)

            def normed_out(q):
                act.wait_ge(s_x2t, q + 1)
                act.activation(XN2T[:, q % 2, :], xt_bank[q][:, :], ACT.Copy).then_inc(s_x2ev, 1)

            def weights_high(i, par):
                act.wait_ge(s_ws[par], 48 * (i + 1))
                act.activation(WE[:, bass.ds((2 * i + par) * EW, 2 * H)],
                               WS[:, par, 0:2, :].rearrange("p k n -> p (k n)"), ACT.Copy)
                act.activation(down_half(2 * i + par, 0),
                               WS[:, par, 2, :].rearrange("p (h n) -> p h n", h=HC), ACT.Copy).then_inc(s_wh[par], 1)

            def values(t, u):
                act.activation(VR[:, u, :], VBf[:, bass.ds(t * VW, VW)], ACT.Copy)

            def shift(u):
                act.activation(shift_m[64:80, u % 2, :], bank[6][0:16, 0:P], ACT.Copy, scale=-1.0).then_inc(s_shift, 1)

            def lead(t, u, i):
                if isinstance(t, int) and t == 1:
                    act.wait_ge(s_mt, 1)
                    shift(0)
                    act.wait_ge(s_lo, 3 * NQ)
                    values(0, 0)

            def follow(t, u, i):
                end = t if isinstance(t, int) else 2
                later = end > 0
                if end == NT - 2:
                    normed_out(1)
                for gp in (0, 1):
                    act.wait_ge(s_st[gp], t + 1)
                    if later:
                        act.wait_ge(s_pl[gp], t)
                    act.activation(P32[:, gp, :], bank[2 + gp][:, :], ACT.Exp).then_inc(s_exp[gp], 1)
                    act.wait_ge(s_exp[gp], t + 1)
                    act.activation(PH[:, u % 2, 512 * gp:512 * gp + 512], P32[:, gp, :], ACT.Copy).then_inc(s_ph[gp], 1)
                    if gp == 0 and end >= 2:
                        output_out(t - 2, u)
                if not (isinstance(t, int) and t == NT - 1):
                    shift(u + 1)
                    values(t + 1, (u + 1) % 4)
                if u % 2 and end != NT - 1:
                    weights_high(i, u // 2)
                if end == NT - 4:
                    rsqrt(s_rv, 1, s_rrs, tiles(BATCHES[0]))
                if end == NT - 3:
                    normed_out(0)

            attention(act, lead, follow)

            output_out(NT - 2, 0)
            output_out(NT - 1, 1)
            rsqrt(s_rv, 2, s_rrs, tiles(BATCHES[1]))
            weights_high(NQ - 1, 1)
            act.wait_ge(s_gin, 1)
            act.activation(m2[:, tiles(BATCHES[0])], m2[:, tiles(BATCHES[0])], ACT.Exp).then_inc(s_gexp, 1)
            for q in BATCHES[1]:
                normed_out(q)
            act.wait_ge(s_gin, 2)
            act.activation(m2[:, tiles(BATCHES[1])], m2[:, tiles(BATCHES[1])], ACT.Exp).then_inc(s_gexp, 1)

            def silu(s, p):
                act.wait_ge(s_gu, s + 1)
                act.activation(SG[:, p, :], bank[p][:, :], ACT.Silu).then_inc(s_silu, 1)

            def high(s, p):
                act.wait_ge(s_h, s + 1)
                act.activation(HH[:, p, 0, :], HF[:, p, :], ACT.Copy).then_inc(s_hh, 1)

            def hidden_out(p, k):
                return act.activation(HT[:, p, k, :], bank[4 + p][:, :].bitcast(F16)[:, H * k:H * k + H], ACT.Copy)

            def ffn_step(s, u, i, gu, th, dn):
                if gu:
                    silu(s, u % 2)
                if th:
                    act.wait_ge(s_ht, s + 1)
                    hidden_out((u + 1) % 2, 0)
                if gu:
                    high(s, u % 2)
                if th:
                    hidden_out((u + 1) % 2, 1).then_inc(s_htev, 1)

            experts(act, ffn_step)

            for q, choices in ((NQ - 1, (0, 1)), (NQ - 2, (1,))):
                act.wait_ge(s_ya[q], 16)
                for k in choices:
                    for t in range(4 * q, 4 * q + 4):
                        part = YA[:, t, D * k:D * k + D]
                        last = act.activation(part, part, ACT.Copy, scale=gw[:, t, k:k + 1])
                    last.then_inc(s_weighed, 1)

        @block.tensor
        def _(pe):
            def mm(o, a, b, start, stop=False):
                return pe.matmul(o, a, b, start=start, stop=stop, skip_group_check=True)

            pe.wait_ge(s_consts, 1)
            pe.wait_ge(s_weights, 16 * N_W)
            for n in range(4):
                tr = pe.transpose(bank[n][:, 0:P], w_nat[:, n, :], ident[:, :])
            tr.then_inc(s_wt, 1)
            pe.wait_ge(s_wperm, 1)
            pe.transpose(bank[4][:, 0:P], woP[:, :], ident[:, :]).then_inc(s_wt, 1)
            pe.wait_ge(s_wperm, 2)
            for n in (0, 1):
                pe.transpose(bank[6][:, n:n + 1], b_row[:, n, :], ident[0:1, 0:1])
            pe.wait_ge(s_wev, 4)
            mm(bank[5][:, 0:P], bvb[:, :], woT[:, :], True, True).then_inc(s_wt, 1)
            pe.wait_ge(s_wev, 5)
            pe.wait_ge(s_bias, 1)

            for t in range(NQ):
                par = t % 2
                pe.wait_ge(s_c[t], 16)
                pe.wait_ge(s_trev, 2 * t)
                for j in range(4):
                    tr = pe.transpose(bank[1][:, P * j:P * j + P], C[:, 4 * t + j, :], ident[:, :])
                tr.then_inc(s_tr, 1)
                pe.wait_ge(s_xn, t + 1)
                for j in range(4):
                    tr = pe.transpose(bank[0][:, P * j:P * j + P], XN[:, par, j, :], ident[:, :])
                tr.then_inc(s_tr, 1)
                if t >= 2:
                    pe.wait_ge(s_lo, 3 * (t - 1))
                pe.wait_ge(s_trev, 2 * t + 1)
                mm(bank[4 + par][:, :], wkT[:, :], cT[:, par, :], True, True).then_inc(s_qkv, 1)
                pe.wait_ge(s_trev, 2 * t + 2)
                mm(bank[2 + par][:, :], wqT[:, :], xT[:, par, :], True, True).then_inc(s_qkv, 1)
                for j in range(4):
                    v = mm(bank[6 + par][:, P * j:P * j + P], cT[:, par, P * j:P * j + P], wvT[:, :], j == 0, True)
                v.then_inc(s_qkv, 1)
            pe.wait_ge(s_consts, N_CONST)

            def turn_output(t, u):
                for b in (0, 1):
                    at = P + P * b
                    tr = pe.transpose(bank[6][0:64, at:at + P], O[:, u % 2, 64 * b:64 * b + 64], ident[:, :])
                tr.then_inc(s_ot, 1)

            def project(t, u):
                pe.wait_ge(s_otev, t + 1)
                mm(bank[4 + u % 2][:, OCOL:OCOL + P], OT[:, u % 2, :], WO[:, :], True, True).then_inc(s_op, 1)

            def turn_normed(q):
                pe.wait_ge(s_xn2, q + 1)
                if q == 1:
                    pe.wait_ge(s_x2ev, q)
                for j in range(4):
                    tr = pe.transpose(xt_bank[q][:, P * j:P * j + P], XN2[:, 4 * q + j, :], ident[:, :])
                tr.then_inc(s_x2t, 1)

            def route(n, q):
                pe.wait_ge(s_x2ev, q + 1 if n else BATCHES[n][-1] + 1)
                for j in range(4):
                    at = E * (4 * (q % 2) + j)
                    lgm = mm(lg_bank[n][:, at:at + E], XN2T[:, q % 2, P * j:P * j + P], wr_sb[:, :], at == 0, True)
                lgm.then_inc(s_lg, 1)

            def count(n):
                pe.wait_ge(s_oh, n + 1)
                ts = tiles(BATCHES[n])
                end = ts.stop + (ts.stop == NT)
                at = lambda t: RKC[n] + E * (t - ts.start)
                mm(rk_bank[n][:, at(ts.start):at(ts.stop)], before[:, :], ohb[:, ts, :].rearrange("p t e -> p (t e)"), n == 1)
                for i in range(end - 1):
                    first = max(i + 1, ts.start)
                    rk = mm(rk_bank[n][:, at(first):at(end)], ones_b[:, :],
                            ohb[:, i, :].unsqueeze(1).to_broadcast([P, end - first, E]), False, True)
                rk.then_inc(s_rk, 1)

            def max_rows(u):
                pe.transpose(bank[6][0:16, 0:P], MX[:, u % 2, :, :].rearrange("p v b -> p (v b)"), ident[:, :])\
                  .then_inc(s_mt, 1)

            def lead(t, u, i):
                first = isinstance(t, int) and t == 0
                pe.wait_ge(s_stack[u], 80 * (i + 1))
                if not first:
                    pe.wait_ge(s_max, t)
                for b in (0, 1):
                    toks = slice(64 * b, 64 * b + 64)
                    mm(bank[b][:, :], identb[:, :], mask_q[:, :].unsqueeze(1).to_broadcast([P, 8, 64]), True)
                    for rp in (0, 1):
                        for g in range(4):
                            at = 64 * (4 * rp + g)
                            sc = mm(bank[b][:, at:at + 64],
                                    QE[:, u, 2 * g + b, 2 * rp:2 * rp + 2, :].rearrange("p r q -> p (r q)"),
                                    KS[:, u, g, toks], False, True)
                    sc.then_inc(s_sc[b], 1)
                if isinstance(t, int) and t == 1:
                    pe.wait_ge(s_lo, 3 * (NQ - 1))
                    max_rows(0)

            def products(t, u):
                tpar = u % 2
                pe.wait_ge(s_pl[1], t + 1)
                if not (isinstance(t, int) and t < 2):
                    pe.wait_ge(s_x2, t - 1)
                for g in range(4):
                    for r in range(4):
                        r1, at = 64 * (r % 2), 36 * (2 * g + r // 2)
                        col, at_v = 256 * g + 64 * r, 36 * (4 * g + r)
                        mm(bank[4 + tpar][r1:r1 + 64, at:at + 36], PH[:, tpar, col:col + 64], VR[:, u % 4, at_v:at_v + 36],
                           g == 0 and r < 2)
                        pv = mm(bank[4 + tpar][r1:r1 + 64, at:at + 18], PL[:, tpar, col:col + 64], VR[:, u % 4, at_v:at_v + 18], False, True)
                pv.then_inc(s_pv, 1)

            def follow(t, u, i):
                pe.wait_ge(s_shift, t + 1)
                end = t if isinstance(t, int) else 2
                if end == NT - 2:
                    pe.wait_ge(s_max, NT)
                if end < NT - 1:
                    max_rows(u + 1)
                if end == NT - 2:
                    turn_normed(1)
                if end == 0:
                    pe.wait_ge(s_lo, 3 * NQ)
                for gp in (0, 1):
                    if gp == 1 and end >= 2:
                        pe.wait_ge(s_o, t - 1)
                    for g2 in (0, 1):
                        for rp in (0, 1):
                            at = 256 * g2 + 128 * rp
                            mm(bank[2 + gp][:, at:at + P], shift_w[:, 4 * rp + 2 * gp + g2, :],
                               shift_m[:, u % 2, :], g2 == 0 and rp == 0)
                    if gp == 1 and end >= 2:
                        turn_output(t - 2, u)
                    for g2 in (0, 1):
                        for b in (0, 1):
                            toks = slice(64 * b, 64 * b + 64)
                            st = mm(bank[2 + gp][64 * b:64 * b + 64, 256 * g2:256 * g2 + 256],
                                    KS[:, u, 2 * gp + g2, toks],
                                    QE[:, u, 2 * (2 * gp + g2) + b, :, :].rearrange("p r q -> p (r q)"), False, True)
                    st.then_inc(s_st[gp], 1)
                if end == NT - 1:
                    count(0)
                if end > 0:
                    products(t - 1, u + 3)
                if end >= 2:
                    project(t - 2, u)
                if end == NT - 3:
                    turn_normed(0)
                if end == NT - 2:
                    route(0, 0)
                    route(0, 1)

            attention(pe, lead, follow)
            pe.wait_ge(s_o, NT - 1)
            turn_output(NT - 2, 0)
            products(NT - 1, 3)
            project(NT - 2, 0)
            pe.wait_ge(s_o, NT)
            turn_output(NT - 1, 1)
            project(NT - 1, 1)
            for q in BATCHES[1]:
                turn_normed(q)
            for q in BATCHES[1]:
                route(1, q)
            count(1)

            def rows_in(u, i, done):
                pe.wait_ge(s_xg[u % R6], arrived[u // R6])
                for k in (0, 1):
                    tr = pe.transpose(bank[6][:, :].bitcast(F16)[:, P * k:P * k + P], XG[:, u % R6, P * k:P * k + P],
                                      ident16[:, :])
                tr.then_inc(done, 1)

            arrived = {}

            base = {}

            def load_bases(first, n, turn):
                for ahead in (0, 1):
                    count = 16 * (turn + 1 + ahead)
                    arrived[ahead] = count if isinstance(turn, int) else pe.snap(count)
                _, values = nc.values_load_multi_w_load_instructions(
                    tile_base[0:1, bass.ds(first, n)], engines=(mybir.EngineType.PE,), min_val=0, max_val=(E - 1) * EW,
                    skip_runtime_bounds_check_because="the table holds min(expert, E - 1) * EW")
                base.update(enumerate(values))

            def gate_up(s, u):
                p = u % 2
                pe.wait_ge(s_xtev, s + 1)
                for n, (half, w) in enumerate(((0, 0), (0, 1), (1, 0))):
                    for gu in (0, 1):
                        g = mm(bank[2 * gu + p][:, :], XGT[:, p, half, :],
                               WE[:, bass.ds(base[u] + (2 * H * w + H * gu), H)], n == 0, n == 2)
                g.then_inc(s_gu, 1)

            def hidden_rows(s, u):
                p = u % 2
                pe.wait_ge(s_hl, s + 2)
                for k in (0, 1):
                    for hc in range(HC):
                        at = H * k + P * hc
                        tr = pe.transpose(bank[4 + p][:, :].bitcast(F16)[:, at:at + P], HH[:, p, k, P * hc:P * hc + P],
                                          ident16[:, :])
                tr.then_inc(s_ht, 1)

            def down(s, u):
                p = u % 2
                pe.wait_ge(s_htev, s + 3)
                for hc in range(HC):
                    at = base[u] + (4 * H + 2 * D * hc)
                    mm(bank[7][:, 0:256], HT[:, p, 0, P * hc:P * hc + P], WE[:, bass.ds(at, 2 * D)], hc == 0)
                    y = mm(bank[7][:, 0:P], HT[:, p, 1, P * hc:P * hc + P], WE[:, bass.ds(at, D)], False, hc == HC - 1)
                y.then_inc(s_y, 1)

            def ffn_step(s, u, i, gu, th, dn):
                if gu:
                    gate_up(s, u)
                if gu and gu != "last":
                    rows_in(u + 1, i, s_xt)
                if th:
                    hidden_rows(s - 1, u - 1)
                if dn and not th:
                    pe.wait_ge(s_yev, FT - 1)
                if dn:
                    down(s - 2, u - 2)

            pe.wait_ge(s_table, 2)
            for par in (0, 1):
                pe.wait_ge(s_wl[par], E // 2)
            arrived[0] = 16
            rows_in(0, 0, s_xt0)
            experts(pe, ffn_step, load_bases)

        @block.vector
        def _(dve):
            step = Chain(dve, s_dve)
            for s_ring, n in ((s_hl, 1), (s_ht, 1), (s_htev, 2), (s_y, 2)):
                dve.sem_inc(s_ring, n)
            dve.memset(ones_f[:, :], 1.0).then_inc(s_dconsts, 1)
            dve.wait_ge(s_dconsts, 1)
            def norm_stats(src, q):
                for t in range(4 * q, 4 * q + 4):
                    last = dve.bn_stats(stats[:, t, :], src[:, t, :])
                step(last)

            def norm_var(ts, ready):
                for t in range(ts.start, ts.stop):
                    last = dve.bn_aggr(mv[:, t, :], stats[:, t, :])
                step(last)
                dve.tensor_scalar(ve[:, ts], mv[:, ts, 1], EPS, None, ALU.add).then_inc(ready, 1)

            def norm_scale(ts, estimate, n):
                dve.wait_ge(estimate, n)
                step(dve.tensor_tensor(nt[:, ts], r0[:, ts], r0[:, ts], ALU.mult))
                step(dve.tensor_tensor(nt[:, ts], nt[:, ts], ve[:, ts], ALU.mult))
                step(dve.tensor_scalar(nt[:, ts], nt[:, ts], -0.5, 1.5, ALU.mult, ALU.add))
                step(dve.tensor_tensor(nt[:, ts], nt[:, ts], r0[:, ts], ALU.mult))

            def norm_apply(dst, src, q, done):
                for j in range(4):
                    t = 4 * q + j
                    last = dve.tensor_scalar(dst[:, j, :], src[:, t, :], mv[:, t, 0:1], nt[:, t:t + 1],
                                             ALU.subtract, ALU.mult)
                last.then_inc(done, 1)

            dve.wait_ge(s_weights, 16 * N_W)
            dve.tensor_copy(woP[:, :].rearrange("o (r g d) -> o r g d", r=2, d=HD),
                            w_nat[:, 3, :].rearrange("o (g r d) -> o r g d", r=2, d=HD)).then_inc(s_wperm, 1)
            for n, scale in enumerate((SCALE, 1.0)):
                dve.tensor_scalar(b_row[:, n, :].rearrange("o (d r g) -> o g r d", d=HD, r=4),
                                  b_nat[:, n, :].rearrange("o (g r d) -> o g r d", d=HD, r=4), scale, None, ALU.mult)
            dve.tensor_scalar(bvb[:, :], ones_f[:, :], bv_c[:, 0:1], None, ALU.mult).then_inc(s_wperm, 1)
            for t in range(NQ):
                dve.wait_ge(s_x[t], 16)
                norm_stats(X, t)
            norm_var(slice(0, NT), s_var)
            dve.wait_ge(s_wt, 3)
            dve.tensor_copy(b_col[:, :], bank[6][:, 0:2])
            dve.tensor_tensor(bias_row[:, :], bank[5][:, 0:P], bo_b[:, :], ALU.add).then_inc(s_bias, 1)
            dve.wait_ge(s_bias, 1)
            norm_scale(slice(0, NT), s_rs, 1)
            norm_apply(XN[:, 0, :, :], X, 0, s_xn)
            dve.memset(QE[:, :, :, :, :].rearrange("p a r g t -> p (a r g t)").bitcast(F32), 0.0).then_inc(s_dconsts, 1)
            dve.memset(KS[:, :, :, :].rearrange("p a g t -> p (a g t)").bitcast(F32), 0.0).then_inc(s_dconsts, 1)
            norm_apply(XN[:, 1, :, :], X, 1, s_xn)

            def low(t):
                par = t % 2
                for i, n in enumerate((1, 0)):
                    dve.wait_ge(s_hi, 3 * t + i + 1)
                    dve.scalar_tensor_tensor(out=QK[:, par, n, 1, :], in0=bank[2 + 2 * n + par][:, :],
                                             scalar=b_col[:, n:n + 1], in1=QK[:, par, n, 0, :],
                                             op0=ALU.add, op1=ALU.subtract).then_inc(s_lo, 1)
                dve.wait_ge(s_hi, 3 * t + 3)
                dve.wait_ge(s_consts, N_CONST)
                for b in (0, 1):
                    rows = slice(64 * b, 64 * b + 64)
                    last = dve.tensor_tensor(VB[rows, 4 * t:4 * t + 4, :, 18 + 9 * b:26 + 9 * b],
                                             bank[6 + par][rows, :].rearrange("p (t h d) -> p t h d", t=4, d=HD),
                                             VB[rows, 4 * t:4 * t + 4, :, 9 * b:9 * b + 8], ALU.subtract)
                last.then_inc(s_lo, 1)

            low(0)
            norm_apply(XN[:, 0, :, :], X, 2, s_xn)
            low(1)
            norm_apply(XN[:, 1, :, :], X, 3, s_xn)
            dve.wait_ge(s_xn, NQ)
            low(2)
            dve.wait_ge(s_tanh, 1)
            step(dve.tensor_scalar(bias_row[:, :], bias_row[:, :], tg[:, 0:1], None, ALU.mult))
            step(dve.tensor_tensor(X[:, :, :], X[:, :, :], bias_row[:, :].unsqueeze(1).to_broadcast([P, NT, D]), ALU.add))
            low(3)
            dve.tensor_copy(jrow[:, :], jint[:, :])
            dve.tensor_scalar(tie[:, :], eint[:, :], -1.0, float(E), ALU.mult, ALU.add)
            step(dve.tensor_scalar(ebase[:, :], eint[:, :], float(N), None, ALU.mult))

            X2f, Xf = (v[:, :, :].rearrange("p t n -> p (t n)") for v in (X2, X))
            statsf = stats[:, :, :].rearrange("p t n -> p (t n)")

            def after_attention(t, u):
                dve.wait_ge(s_op, t + 1)
                at = bass.ds(t * P, P)
                dve.scalar_tensor_tensor(out=X2f[:, at], in0=bank[4 + u % 2][:, OCOL:OCOL + P],
                                         scalar=tg[:, 0:1], in1=Xf[:, at], op0=ALU.mult, op1=ALU.add).then_inc(s_x2, 1)
                dve.wait_ge(s_x2, t + 1)
                dve.bn_stats(statsf[:, bass.ds(t * 6, 6)], X2f[:, at]).then_inc(s_stats, 1)

            def first_of(oh, vals, top, ts):
                n = ts.stop - ts.start
                b = lambda v: v[:, ts].unsqueeze(2).to_broadcast([P, n, E])
                step(dve.tensor_reduce(top[:, ts], vals[:, ts, :], AX.X, ALU.max))
                step(dve.tensor_tensor(oh[:, ts, :], vals[:, ts, :], b(top), ALU.is_equal))
                step(dve.tensor_tensor(oh[:, ts, :], oh[:, ts, :], tie[:, :].unsqueeze(1).to_broadcast([P, n, E]), ALU.mult))
                step(dve.tensor_reduce(tm[:, ts], oh[:, ts, :], AX.X, ALU.max))
                step(dve.tensor_tensor(oh[:, ts, :], oh[:, ts, :], b(tm), ALU.is_equal))

            def expert_rows(q):
                t4 = tiles((q,))
                step(dve.tensor_copy(XHL[q][:, 0, :, 0:D], XN2[:, t4, :]))
                step(dve.tensor_tensor(XHL[q][:, 0, :, D:2 * D], XN2[:, t4, :], XHL[q][:, 0, :, 0:D], ALU.subtract))
                dve.tensor_copy(XHL[q][:, 1, :, 0:2 * D], XHL[q][:, 0, :, 0:2 * D]).then_inc(s_xhl, 1)

            def choose(n):
                ts = tiles(BATCHES[n])
                nt_ = ts.stop - ts.start
                dve.wait_ge(s_lg, BATCHES[n][-1] + 1)
                step(dve.tensor_tensor(lg[:, ts, :], lg_bank[n][:, 0:E * nt_].rearrange("p (t e) -> p t e", e=E),
                                       br_b[:, :].unsqueeze(1).to_broadcast([P, nt_, E]), ALU.add))
                first_of(oh1, lg, m1, ts)
                step(dve.scalar_tensor_tensor(out=le[:, ts, :], in0=oh1[:, ts, :], scalar=NEG, in1=lg[:, ts, :],
                                              op0=ALU.mult, op1=ALU.add))
                first_of(oh2, le, m2, ts)
                dve.tensor_tensor(ohb[:, ts, :], oh1[:, ts, :], oh2[:, ts, :], ALU.add).then_inc(s_oh, 1)
                dve.tensor_tensor(m2[:, ts], m2[:, ts], m1[:, ts], ALU.subtract).then_inc(s_gin, 1)

            def places(n):
                ts = tiles(BATCHES[n])
                nt_ = ts.stop - ts.start
                dve.wait_ge(s_rk, n + 1)
                step(dve.tensor_tensor(rank[:, ts, :], rk_bank[n][:, RKC[n]:RKC[n] + E * nt_].rearrange("p (t e) -> p t e", e=E),
                                       ebase[:, :].unsqueeze(1).to_broadcast([P, nt_, E]), ALU.add))
                for k, o in enumerate((oh1, oh2)):
                    step(dve.tensor_tensor(le[:, ts, :], o[:, ts, :], rank[:, ts, :], ALU.mult))
                    step(dve.tensor_reduce(posf[:, k, ts], le[:, ts, :], AX.X, ALU.add))
                if ts.stop == NT:
                    step(dve.tensor_copy(runs[:, :], rk_bank[n][:, E * nt_:E * nt_ + E]))
                dve.tensor_copy(pos[:, :, ts], posf[:, :, ts]).then_inc(s_pos, 1)

            def gate_weights(n):
                ts = tiles(BATCHES[n])
                dve.wait_ge(s_gexp, n + 1)
                step(dve.tensor_scalar(m1[:, ts], m2[:, ts], 1.0, None, ALU.add))
                step(dve.reciprocal(m1[:, ts], m1[:, ts]))
                step(dve.tensor_scalar(gw[:, ts, 0], m1[:, ts], tg[:, 1:2], None, ALU.mult))
                step(dve.tensor_tensor(gw[:, ts, 1], m2[:, ts], gw[:, ts, 0], ALU.mult))

            def lead(t, u, i):
                for b in (0, 1):
                    dve.wait_ge(s_sc[b], t + 1)
                    last = dve.tensor_reduce(MX[:, u % 2, :, b], bank[b][:, :].rearrange("p (v k) -> p v k", k=64),
                                             AX.X, ALU.max)
                last.then_inc(s_max, 1)


            def normalise(t, u):
                dve.wait_ge(s_pv, t + 1)
                pv = bank[4 + u % 2][:, 0:288].rearrange("p (v w) -> p v w", w=36)
                step(dve.tensor_reduce(SM[:, :, :], pv.rearrange("p v (k w) -> p v w k", k=2), AX.X, ALU.add))
                sm = SM[:, :, :].rearrange("p v (b w) -> p v b w", b=2)
                step(dve.reciprocal(RS[:, :, :], sm[:, :, :, 8]))
                dve.tensor_tensor(O[:, u % 2, :].rearrange("p (b v d) -> p v b d", b=2, d=HD),
                                  sm[:, :, :, 0:8], RS[:, :, :].unsqueeze(3).to_broadcast([P, 8, 2, HD]),
                                  ALU.mult).then_inc(s_o, 1)

            def follow(t, u, i):
                end = t if isinstance(t, int) else 2
                if end == NT - 4:
                    dve.wait_ge(s_stats, tiles(BATCHES[0]).stop)
                    norm_var(tiles(BATCHES[0]), s_rv)
                if end == NT - 3:
                    norm_scale(tiles(BATCHES[0]), s_rrs, 1)
                    norm_apply(XN2[:, 0:4, :], X2, 0, s_xn2)
                if end == NT - 1:
                    dve.wait_ge(s_xn2, 2)
                    expert_rows(0)
                for gp in (0, 1):
                    half = slice(512 * gp, 512 * gp + 512)
                    dve.wait_ge(s_ph[gp], t + 1)
                    dve.tensor_tensor(PL[:, u % 2, half], P32[:, gp, :], PH[:, u % 2, half], ALU.subtract).then_inc(s_pl[gp], 1)
                if end > 0:
                    if end > 1:
                        dve.wait_ge(s_o, t - 1)
                    normalise(t - 1, u + 3)
                if end > 1:
                    after_attention(t - 2, u)
                if end == NT - 3:
                    norm_apply(XN2[:, 4:8, :], X2, 1, s_xn2)
                if end == NT - 2:
                    choose(0)
                if end == NT - 1:
                    places(0)

            attention(LoopChain(dve, step, 8, 2), lead, follow)
            dve.wait_ge(s_o, NT - 1)
            normalise(NT - 1, 1)
            after_attention(NT - 2, 0)
            after_attention(NT - 1, 1)
            dve.wait_ge(s_stats, NT)
            norm_var(tiles(BATCHES[1]), s_rv)
            expert_rows(1)
            norm_scale(tiles(BATCHES[1]), s_rrs, 2)
            for q in BATCHES[1]:
                norm_apply(XN2[:, 4 * q:4 * q + 4, :], X2, q, s_xn2)
            dve.wait_ge(s_xn2, NQ)
            dve.wait_ge(s_ids, NQ)
            expert_rows(2)
            expert_rows(3)
            choose(1)
            places(1)
            gate_weights(0)
            gate_weights(1)

            one = lambda v: v[0:1, :]
            step(dve.tensor_scalar(cnt_i[:, :], one(runs), float(P - 1), None, ALU.add))
            step(dve.tensor_scalar(cnt_i[:, :], cnt_i[:, :], 7, None, ALU.logical_shift_right))
            step(dve.tensor_copy(cnt_f[:, :], cnt_i[:, :]))
            step(dve.tensor_tensor_scan(tiles_to[:, :], ones_f[0:1, 0:E], cnt_f[:, :], 0.0, ALU.mult, ALU.add))
            jb = jrow[:, :].unsqueeze(2).to_broadcast([1, FT, E])
            eb = lambda v: v[:, :].unsqueeze(1).to_broadcast([1, FT, E])
            step(dve.tensor_tensor(jge[:, :, :], jb, eb(tiles_to), ALU.is_ge))
            step(dve.tensor_reduce(jex[:, :], jge[:, :, :], AX.X, ALU.add))
            step(dve.tensor_tensor(jge[:, :, :], jge[:, :, :], eb(cnt_f), ALU.mult))
            step(dve.tensor_reduce(jbk[:, :], jge[:, :, :], AX.X, ALU.add))
            step(dve.tensor_tensor(jbk[:, :], jrow[:, :], jbk[:, :], ALU.subtract))
            step(dve.tensor_scalar(jbk[:, :], jbk[:, :], float(P), None, ALU.mult))
            dve.scalar_tensor_tensor(out=tile_row[:, 0:FT], in0=jex[:, :], scalar=float(N), in1=jbk[:, :],
                                     op0=ALU.mult, op1=ALU.add).then_inc(s_table, 1)
            dve.tensor_scalar(tile_base[:, 0:FT], jex[:, :], float(E - 1), float(EW), ALU.min, ALU.mult).then_inc(s_table, 1)

            def rows_out(u):
                dve.tensor_copy(XGT[:, u % 2, :, :].rearrange("p k n -> p (k n)"), bank[6][:, :].bitcast(F16)[:, 0:256])\
                   .then_inc(s_xtev, 1)

            def ffn_step(s, u, i, gu, th, dn):
                p = u % 2
                if gu and gu != "last":
                    dve.wait_ge(s_xt, s + 1)
                    rows_out(u + 1)
                if gu:
                    dve.wait_ge(s_silu, s + 1)
                    dve.tensor_tensor(HF[:, p, :], SG[:, p, :], bank[2 + p][:, :], ALU.mult).then_inc(s_h, 1)
                if dn:
                    dve.wait_ge(s_y, s + 1)
                    dve.tensor_reduce(YS[:, (u - 2) % R6, :], bank[7][:, 0:2 * P].rearrange("p (k n) -> p n k", k=2),
                                      AX.X, ALU.add).then_inc(s_yev, 1)
                if gu:
                    dve.wait_ge(s_hh, s + 1)
                    dve.tensor_tensor(HH[:, p, 1, :], HF[:, p, :], HH[:, p, 0, :], ALU.subtract).then_inc(s_hl, 1)

            dve.wait_ge(s_xt0, 1)
            rows_out(0)
            experts(dve, ffn_step)

            def add_weighed(q, k):
                for t in range(4 * q, 4 * q + 4):
                    last = dve.scalar_tensor_tensor(out=X2[:, t, :], in0=YA[:, t, D * k:D * k + D],
                                                    scalar=gw[:, t, k:k + 1], in1=X2[:, t, :],
                                                    op0=ALU.mult, op1=ALU.add)
                return last

            for q in range(NQ - 2):
                dve.wait_ge(s_ya[q], 16)
                step(add_weighed(q, 0))
                add_weighed(q, 1).then_inc(s_fin, 1)
            q = NQ - 2
            dve.wait_ge(s_ya[q], 16)
            step(add_weighed(q, 0))
            dve.wait_ge(s_weighed, K + 1)
            quarter = slice(4 * q, 4 * q + 4)
            last = dve.tensor_tensor(X2[:, quarter, :], X2[:, quarter, :], YA[:, quarter, D:2 * D], ALU.add)
            last.then_inc(s_fin, 1)


_INS = ['x', 'ctx_1024', 'g_xattn', 'g_ffn', 'L0_xattn_wq', 'L0_xattn_bq', 'L0_xattn_wk', 'L0_xattn_bk', 'L0_xattn_wv',
        'L0_xattn_bv', 'L0_xattn_wo', 'L0_xattn_bo', 'L0_ffn_Wr', 'L0_ffn_br', 'L0_ffn_Wg', 'L0_ffn_Wu', 'L0_ffn_Wd']


def kernel(**inputs):
    import numpy as _np
    import concourse.bacc as _bacc
    from concourse import mybir as _mybir
    from concourse.bass_utils import run_bass_kernel_spmd as _run

    nc = _bacc.Bacc("TRN2", target_bir_lowering=False, num_devices=1)
    arrays, args = {}, []
    for name in _INS:
        a = _np.ascontiguousarray(inputs[name])
        arrays[f"in_{name}_dram"] = a
        args.append(nc.dram_tensor(f"in_{name}_dram", a.shape, _mybir.dt.from_np(a.dtype), kind="ExternalInput").ap())
    shape = inputs["x"].shape
    out = nc.dram_tensor("out_0_dram", shape, _mybir.dt.float32, kind="ExternalOutput").ap()
    flamingo_gated_block(nc, *args, out)
    r = _run(nc, [arrays], core_ids=[0])
    return r.results[0]["out_0_dram"]
```
